# Optimizing a Trainium2 kernel written in Bass

```python
import numpy as np
import jax
import jax.numpy as jnp

def _softmax(x, axis=-1):
    return jax.nn.softmax(x, axis=axis)

def _gelu(x):
    return jax.nn.gelu(x, approximate=True)

def _silu(x):
    return jax.nn.silu(x)

def _sigmoid(x):
    return jax.nn.sigmoid(x)

def _layernorm(x, axis=-1, eps=1e-05):
    m = jnp.mean(x, axis=axis, keepdims=True)
    v = jnp.var(x, axis=axis, keepdims=True)
    return (x - m) / jnp.sqrt(v + eps)

def _scatter_add(tgt, idx, src, axis=0):
    return tgt.at[idx].add(src)

def _segment_sum(src, seg, n):
    return jax.ops.segment_sum(src, seg, n)
kernel_name = 'mk_dlrm_tower_d1_rec_r8_2ba5e7'

def setup_inputs(seed: int=0):
    np.random.seed(seed)
    _w = jnp.asarray

    def _rec_inputs():
        import jax
        import jax.numpy as jnp
        _tk = jax.random.key(seed)
        dense_ctx = jax.random.normal(jax.random.fold_in(_tk, 190), (512, 16), jnp.float32)
        ids = jnp.stack([jax.random.randint(jax.random.fold_in(_tk, 200 + f), (512,), 0, v, jnp.int32) for f, v in enumerate([1000, 125000, 1000, 125000, 12500, 1000, 125000, 12500, 1250, 12500, 125000, 125000, 12500, 125000, 1000, 12500, 1250, 12500, 1250, 125000, 1250, 125000, 125000, 12500, 125000, 1250, 1000, 12500, 125000, 1250, 125000, 12500, 1250, 1250, 1250, 1000, 1000, 1000, 125000])], axis=1)
        tbl_0 = 0.05 * jax.random.normal(jax.random.fold_in(_tk, 500 + 0), (1000, 16), jnp.float32)
        tbl_1 = 0.05 * jax.random.normal(jax.random.fold_in(_tk, 500 + 1), (125000, 16), jnp.float32)
        tbl_2 = 0.05 * jax.random.normal(jax.random.fold_in(_tk, 500 + 2), (1000, 16), jnp.float32)
        tbl_3 = 0.05 * jax.random.normal(jax.random.fold_in(_tk, 500 + 3), (125000, 16), jnp.float32)
        tbl_4 = 0.05 * jax.random.normal(jax.random.fold_in(_tk, 500 + 4), (12500, 16), jnp.float32)
        tbl_5 = 0.05 * jax.random.normal(jax.random.fold_in(_tk, 500 + 5), (1000, 16), jnp.float32)
        tbl_6 = 0.05 * jax.random.normal(jax.random.fold_in(_tk, 500 + 6), (125000, 16), jnp.float32)
        tbl_7 = 0.05 * jax.random.normal(jax.random.fold_in(_tk, 500 + 7), (12500, 16), jnp.float32)
        tbl_8 = 0.05 * jax.random.normal(jax.random.fold_in(_tk, 500 + 8), (1250, 16), jnp.float32)
        tbl_9 = 0.05 * jax.random.normal(jax.random.fold_in(_tk, 500 + 9), (12500, 16), jnp.float32)
        tbl_10 = 0.05 * jax.random.normal(jax.random.fold_in(_tk, 500 + 10), (125000, 16), jnp.float32)
        tbl_11 = 0.05 * jax.random.normal(jax.random.fold_in(_tk, 500 + 11), (125000, 16), jnp.float32)
        tbl_12 = 0.05 * jax.random.normal(jax.random.fold_in(_tk, 500 + 12), (12500, 16), jnp.float32)
        tbl_13 = 0.05 * jax.random.normal(jax.random.fold_in(_tk, 500 + 13), (125000, 16), jnp.float32)
        tbl_14 = 0.05 * jax.random.normal(jax.random.fold_in(_tk, 500 + 14), (1000, 16), jnp.float32)
        tbl_15 = 0.05 * jax.random.normal(jax.random.fold_in(_tk, 500 + 15), (12500, 16), jnp.float32)
        tbl_16 = 0.05 * jax.random.normal(jax.random.fold_in(_tk, 500 + 16), (1250, 16), jnp.float32)
        tbl_17 = 0.05 * jax.random.normal(jax.random.fold_in(_tk, 500 + 17), (12500, 16), jnp.float32)
        tbl_18 = 0.05 * jax.random.normal(jax.random.fold_in(_tk, 500 + 18), (1250, 16), jnp.float32)
        tbl_19 = 0.05 * jax.random.normal(jax.random.fold_in(_tk, 500 + 19), (125000, 16), jnp.float32)
        tbl_20 = 0.05 * jax.random.normal(jax.random.fold_in(_tk, 500 + 20), (1250, 16), jnp.float32)
        tbl_21 = 0.05 * jax.random.normal(jax.random.fold_in(_tk, 500 + 21), (125000, 16), jnp.float32)
        tbl_22 = 0.05 * jax.random.normal(jax.random.fold_in(_tk, 500 + 22), (125000, 16), jnp.float32)
        tbl_23 = 0.05 * jax.random.normal(jax.random.fold_in(_tk, 500 + 23), (12500, 16), jnp.float32)
        tbl_24 = 0.05 * jax.random.normal(jax.random.fold_in(_tk, 500 + 24), (125000, 16), jnp.float32)
        tbl_25 = 0.05 * jax.random.normal(jax.random.fold_in(_tk, 500 + 25), (1250, 16), jnp.float32)
        tbl_26 = 0.05 * jax.random.normal(jax.random.fold_in(_tk, 500 + 26), (1000, 16), jnp.float32)
        tbl_27 = 0.05 * jax.random.normal(jax.random.fold_in(_tk, 500 + 27), (12500, 16), jnp.float32)
        tbl_28 = 0.05 * jax.random.normal(jax.random.fold_in(_tk, 500 + 28), (125000, 16), jnp.float32)
        tbl_29 = 0.05 * jax.random.normal(jax.random.fold_in(_tk, 500 + 29), (1250, 16), jnp.float32)
        tbl_30 = 0.05 * jax.random.normal(jax.random.fold_in(_tk, 500 + 30), (125000, 16), jnp.float32)
        tbl_31 = 0.05 * jax.random.normal(jax.random.fold_in(_tk, 500 + 31), (12500, 16), jnp.float32)
        tbl_32 = 0.05 * jax.random.normal(jax.random.fold_in(_tk, 500 + 32), (1250, 16), jnp.float32)
        tbl_33 = 0.05 * jax.random.normal(jax.random.fold_in(_tk, 500 + 33), (1250, 16), jnp.float32)
        tbl_34 = 0.05 * jax.random.normal(jax.random.fold_in(_tk, 500 + 34), (1250, 16), jnp.float32)
        tbl_35 = 0.05 * jax.random.normal(jax.random.fold_in(_tk, 500 + 35), (1000, 16), jnp.float32)
        tbl_36 = 0.05 * jax.random.normal(jax.random.fold_in(_tk, 500 + 36), (1000, 16), jnp.float32)
        tbl_37 = 0.05 * jax.random.normal(jax.random.fold_in(_tk, 500 + 37), (1000, 16), jnp.float32)
        tbl_38 = 0.05 * jax.random.normal(jax.random.fold_in(_tk, 500 + 38), (125000, 16), jnp.float32)
        _rk = jax.random.fold_in(_tk, 7)
        W_top1 = 0.0606339 * jax.random.normal(jax.random.fold_in(_tk, 801), (272, 512), jnp.float32)
        W_top2 = 0.0441942 * jax.random.normal(jax.random.fold_in(_tk, 802), (512, 256), jnp.float32)
        W_top3 = 0.0625 * jax.random.normal(jax.random.fold_in(_tk, 803), (256, 1), jnp.float32)
        b_top1 = jnp.zeros((512,), jnp.float32)
        b_top2 = jnp.zeros((256,), jnp.float32)
        return (dense_ctx, ids, tbl_0, tbl_1, tbl_2, tbl_3, tbl_4, tbl_5, tbl_6, tbl_7, tbl_8, tbl_9, tbl_10, tbl_11, tbl_12, tbl_13, tbl_14, tbl_15, tbl_16, tbl_17, tbl_18, tbl_19, tbl_20, tbl_21, tbl_22, tbl_23, tbl_24, tbl_25, tbl_26, tbl_27, tbl_28, tbl_29, tbl_30, tbl_31, tbl_32, tbl_33, tbl_34, tbl_35, tbl_36, tbl_37, tbl_38, W_top1, b_top1, W_top2, b_top2, W_top3)
    dense_ctx, ids, tbl_0, tbl_1, tbl_2, tbl_3, tbl_4, tbl_5, tbl_6, tbl_7, tbl_8, tbl_9, tbl_10, tbl_11, tbl_12, tbl_13, tbl_14, tbl_15, tbl_16, tbl_17, tbl_18, tbl_19, tbl_20, tbl_21, tbl_22, tbl_23, tbl_24, tbl_25, tbl_26, tbl_27, tbl_28, tbl_29, tbl_30, tbl_31, tbl_32, tbl_33, tbl_34, tbl_35, tbl_36, tbl_37, tbl_38, W_top1, b_top1, W_top2, b_top2, W_top3 = _rec_inputs()

    def _L0_rec_setup():
        import jax, jax.numpy as jnp
        import numpy as np
        key = jax.random.key(seed)
        k1, k2, k3 = jax.random.split(key, 3)
        B, M, D = (512, 39, 16)
        H = [128, 128]
        x = jax.random.normal(k1, (B, M, D), dtype=jnp.float32)
        W0 = jax.random.normal(k2, (1, M * M, H[0]), dtype=jnp.float32) * 0.05
        W1 = jax.random.normal(k3, (1, M * H[0], H[1]), dtype=jnp.float32) * 0.05
        return {'x': x, 'W0': W0, 'W1': W1}
    _L0_rec_all = _L0_rec_setup()
    _L0_rec_in = {k: v for k, v in _L0_rec_all.items() if k in ('W0', 'W1')}
    del _L0_rec_all
    return {'dense_ctx': dense_ctx, 'ids': ids, 'tbl_0': tbl_0, 'tbl_1': tbl_1, 'tbl_2': tbl_2, 'tbl_3': tbl_3, 'tbl_4': tbl_4, 'tbl_5': tbl_5, 'tbl_6': tbl_6, 'tbl_7': tbl_7, 'tbl_8': tbl_8, 'tbl_9': tbl_9, 'tbl_10': tbl_10, 'tbl_11': tbl_11, 'tbl_12': tbl_12, 'tbl_13': tbl_13, 'tbl_14': tbl_14, 'tbl_15': tbl_15, 'tbl_16': tbl_16, 'tbl_17': tbl_17, 'tbl_18': tbl_18, 'tbl_19': tbl_19, 'tbl_20': tbl_20, 'tbl_21': tbl_21, 'tbl_22': tbl_22, 'tbl_23': tbl_23, 'tbl_24': tbl_24, 'tbl_25': tbl_25, 'tbl_26': tbl_26, 'tbl_27': tbl_27, 'tbl_28': tbl_28, 'tbl_29': tbl_29, 'tbl_30': tbl_30, 'tbl_31': tbl_31, 'tbl_32': tbl_32, 'tbl_33': tbl_33, 'tbl_34': tbl_34, 'tbl_35': tbl_35, 'tbl_36': tbl_36, 'tbl_37': tbl_37, 'tbl_38': tbl_38, 'W_top1': W_top1, 'b_top1': b_top1, 'W_top2': W_top2, 'b_top2': b_top2, 'W_top3': W_top3, 'L0_rec_W0': _L0_rec_in['W0'], 'L0_rec_W1': _L0_rec_in['W1']}

def reference(dense_ctx, ids, tbl_0, tbl_1, tbl_2, tbl_3, tbl_4, tbl_5, tbl_6, tbl_7, tbl_8, tbl_9, tbl_10, tbl_11, tbl_12, tbl_13, tbl_14, tbl_15, tbl_16, tbl_17, tbl_18, tbl_19, tbl_20, tbl_21, tbl_22, tbl_23, tbl_24, tbl_25, tbl_26, tbl_27, tbl_28, tbl_29, tbl_30, tbl_31, tbl_32, tbl_33, tbl_34, tbl_35, tbl_36, tbl_37, tbl_38, W_top1, b_top1, W_top2, b_top2, W_top3, L0_rec_W0, L0_rec_W1):
    import jax
    import jax.numpy as jnp

    def _L0_rec_ref(x, W0, W1):
        import jax, jax.numpy as jnp
        import numpy as np
        m = x.shape[1]
        x0 = x
        xk = x
        outs = []
        for W in (W0, W1):
            Hk = xk.shape[1]
            Hn = W.shape[-1]
            Wr = W.reshape(m, Hk, Hn)
            xk = jnp.einsum('bid,bjd,ijh->bhd', x0, xk, Wr)
            outs.append(xk)
        result = jnp.concatenate(outs, axis=1)
        return jnp.sum(result, axis=-1)
    e = jnp.stack([tbl_0[ids[:, 0]], tbl_1[ids[:, 1]], tbl_2[ids[:, 2]], tbl_3[ids[:, 3]], tbl_4[ids[:, 4]], tbl_5[ids[:, 5]], tbl_6[ids[:, 6]], tbl_7[ids[:, 7]], tbl_8[ids[:, 8]], tbl_9[ids[:, 9]], tbl_10[ids[:, 10]], tbl_11[ids[:, 11]], tbl_12[ids[:, 12]], tbl_13[ids[:, 13]], tbl_14[ids[:, 14]], tbl_15[ids[:, 15]], tbl_16[ids[:, 16]], tbl_17[ids[:, 17]], tbl_18[ids[:, 18]], tbl_19[ids[:, 19]], tbl_20[ids[:, 20]], tbl_21[ids[:, 21]], tbl_22[ids[:, 22]], tbl_23[ids[:, 23]], tbl_24[ids[:, 24]], tbl_25[ids[:, 25]], tbl_26[ids[:, 26]], tbl_27[ids[:, 27]], tbl_28[ids[:, 28]], tbl_29[ids[:, 29]], tbl_30[ids[:, 30]], tbl_31[ids[:, 31]], tbl_32[ids[:, 32]], tbl_33[ids[:, 33]], tbl_34[ids[:, 34]], tbl_35[ids[:, 35]], tbl_36[ids[:, 36]], tbl_37[ids[:, 37]], tbl_38[ids[:, 38]]], axis=1)
    z = _L0_rec_ref(e, L0_rec_W0, L0_rec_W1)
    z = z.reshape(z.shape[0], -1)
    h = jnp.concatenate([z, dense_ctx], axis=1)
    h = jnp.maximum(h @ W_top1 + b_top1, 0.0)
    h = jnp.maximum(h @ W_top2 + b_top2, 0.0)
    y = h @ W_top3
    return y

_drawn_inputs = setup_inputs


def setup_inputs(seed=0):
    import zlib

    import numpy as np

    out = dict(_drawn_inputs(seed))
    spreads = {'b_top1': (0.0, 0.1), 'b_top2': (0.0, 0.1)}
    factors = {'tbl_0': 4.759,
     'tbl_1': 5.236,
     'tbl_2': 4.703,
     'tbl_3': 4.99,
     'tbl_4': 5.267,
     'tbl_5': 5.099,
     'tbl_6': 4.796,
     'tbl_7': 5.309,
     'tbl_8': 5.497,
     'tbl_9': 4.533,
     'tbl_10': 5.277,
     'tbl_11': 4.873,
     'tbl_12': 4.748,
     'tbl_13': 4.472,
     'tbl_14': 4.839,
     'tbl_15': 4.943,
     'tbl_16': 5.23,
     'tbl_17': 4.85,
     'tbl_18': 5.307,
     'tbl_19': 5.683,
     'tbl_20': 4.85,
     'tbl_21': 5.357,
     'tbl_22': 4.916,
     'tbl_23': 5.132,
     'tbl_24': 4.661,
     'tbl_25': 5.12,
     'tbl_26': 5.058,
     'tbl_27': 5.118,
     'tbl_28': 4.963,
     'tbl_29': 4.933,
     'tbl_30': 5.044,
     'tbl_31': 4.516,
     'tbl_32': 4.983,
     'tbl_33': 4.996,
     'tbl_34': 4.891,
     'tbl_35': 5.225,
     'tbl_36': 4.714,
     'tbl_37': 5.379,
     'tbl_38': 5.062,
     'L0_rec_W1': 5.304}
    for name, (base, spread) in spreads.items():
        noise = np.random.default_rng([zlib.crc32(name.encode()), seed]).standard_normal(out[name].shape)
        drawn = base * np.exp(spread * noise) if base else spread * noise
        out[name] = jnp.asarray(drawn.astype(out[name].dtype))
    for name, factor in factors.items():
        out[name] = (out[name] * factor).astype(out[name].dtype)
    return out
```

```python
from contextlib import ExitStack

import numpy as np

import concourse.bass as bass
from concourse import mybir

ALU = mybir.AluOpType
ACT = mybir.ActivationFunctionType
F32 = mybir.dt.float32
F32R = mybir.dt.float32r
BF16 = mybir.dt.bfloat16
I32 = mybir.dt.int32

P = 128
FIELDS = 39
DIM = 16
BATCH = 512
HALF = 20
UNIT = 64
UNITS = BATCH // UNIT
BLOCK = 32
BLOCKS = BATCH // BLOCK
GROUP = 128
GROUPS = BATCH // GROUP
COLS = BLOCK * DIM
SUB = P // DIM
SUBS = BLOCK // SUB
WIDE = FIELDS + 1
TILES = 6
LEFT = FIELDS * (FIELDS + 1) // 2 - TILES * P
QUAD = 32
H1, H2 = 512, 256


def first_of_pair():
    return [p % FIELDS for p in range(P)]


def pair_tiles():
    first = first_of_pair()
    room = {i: TILES * first.count(i) for i in range(FIELDS)}
    partners = {i: [i] if i >= LEFT else [] for i in range(FIELDS)}
    need = {i: room[i] - len(partners[i]) for i in range(FIELDS)}
    open_fields = list(range(FIELDS))
    while open_fields:
        open_fields.sort(key=lambda i: (need[i], i))
        v = open_fields.pop(0)
        wins = need[v]
        for n, w in enumerate(open_fields):
            if n < wins:
                partners[v].append(w)
            else:
                partners[w].append(v)
                need[w] -= 1
        assert 0 <= wins <= len(open_fields)
    assert all(len(partners[i]) == room[i] for i in range(FIELDS))
    tiles = []
    for _ in range(TILES):
        tiles.append([partners[i].pop() for i in first])
    return tiles


def part_row(field, part):
    return 64 * (field // HALF) + part * HALF + field % HALF


def selections():
    sel = np.zeros((P, TILES + 2, P), np.float32)
    back = np.zeros((P, WIDE), np.float32)
    tiles = [first_of_pair(), *pair_tiles()]
    for n, fields in enumerate(tiles):
        for p, i in enumerate(fields):
            for part in range(3):
                sel[part_row(i, part), n, p] = 1
    for i in range(LEFT):
        for quadrant in range(4):
            for part in range(3):
                sel[part_row(i, part), TILES + 1, QUAD * quadrant + i] = 1
    for i in range(FIELDS):
        for part in range(3):
            back[part_row(i, part), i] = 1
    return sel, back


def pair_rows():
    first, none = first_of_pair(), FIELDS * FIELDS
    ij = np.full((TILES + 1, P), none)
    ji = np.full((TILES + 1, P), none)
    for t, second in enumerate(pair_tiles()):
        for p, (i, j) in enumerate(zip(first, second)):
            ij[t, p] = i * FIELDS + j
            if i != j:
                ji[t, p] = j * FIELDS + i
    for quadrant in range(4):
        for i in range(LEFT):
            ij[TILES, QUAD * quadrant + i] = i * FIELDS + i
    return ij, ji


def build(nc, table, ids, offsets, w0_ij, w0_ji, w1, sel, back, ident, dense, wt1, bt1, wt2, bt2, wt3, out):
    ctx = ExitStack()
    with ctx:
        def sb(name, shape, dt=F32):
            return ctx.enter_context(nc.sbuf_tensor(name, shape, dt))

        def bank(name, shape=(P, COLS), dt=F32):
            return ctx.enter_context(nc.psum_tensor(name, list(shape), dt))

        def sem(name):
            return ctx.enter_context(nc.semaphore(name))

        NPROD, NPART = 3, 4
        ids_sb = sb("ids_sb", [P, UNITS, HALF], I32)
        off_sb = sb("off_sb", [P, HALF], I32)
        rows = sb("rows", [P, UNITS, HALF], I32)
        gathered = sb("gathered", [P, 2, HALF, DIM])
        rest = sb("rest", [P, HALF, DIM])
        parts = sb("parts", [P, 2, DIM, 64], BF16)
        turned = sb("turned", [P, 2, UNIT * DIM], BF16)
        sel_f = sb("sel_f", [P, TILES + 2, P])
        sel_sb = sb("sel_sb", [P, TILES + 2, P], BF16)
        back_f = sb("back_f", [P, WIDE])
        back_sb = sb("back_sb", [P, WIDE], BF16)
        ident_f = sb("ident_f", [P, P])
        ident_b = sb("ident_b", [P, P], BF16)
        w0a = sb("w0a", [P, TILES + 1, P])
        w0b = sb("w0b", [P, TILES + 1, P])
        w0s = sb("w0s", [P, TILES + 1, P])
        w0_hi = sb("w0_hi", [P, TILES + 1, P], F32R)
        w0_lo = sb("w0_lo", [P, TILES, P], F32R)
        first = sb("first", [P, 2, COLS])
        prod = sb("prod", [P, NPROD, COLS])
        prod_hi = sb("prod_hi", [P, NPART, COLS], F32R)
        prod_lo = sb("prod_lo", [P, NPART, COLS], F32R)
        square = sb("square", [P, 2, COLS])
        square_parts = sb("square_parts", [P, 2, COLS], F32R)
        x1 = sb("x1", [P, COLS])
        x1_turned = sb("x1_turned", [P, 2, SUBS, P])
        columns = sb("columns", [P, 2, UNIT // SUB, WIDE])
        diag = sb("diag", [P, 2, UNIT // SUB, SUB * WIDE])
        dots = sb("dots", [P, 2, WIDE, GROUP])
        w1_sb = sb("w1_sb", [P, FIELDS, P])
        dense_sb = sb("dense_sb", [P, GROUPS, DIM])
        dense_t = sb("dense_t", [DIM, BATCH])
        wt1_sb = sb("wt1_sb", [P, 2, H1])
        wtd_sb = sb("wtd_sb", [DIM, H1])
        wt2_sb = sb("wt2_sb", [P, H1 // P, H2])
        wt3_sb = sb("wt3_sb", [P, H2 // P])
        bt1_sb = sb("bt1_sb", [P, H1 // P])
        bt2_sb = sb("bt2_sb", [P, H2 // P])
        z2 = sb("z2", [P, GROUP])
        h1 = sb("h1", [P, H1 // P, GROUP])
        h2 = sb("h2", [P, H2 // P, GROUP])
        y = sb("y", [1, BATCH])

        copies = [bank(f"copies{i}") for i in range(3)]
        sums = bank("sums")
        turn = bank("turn")
        ring = [bank(f"ring{i}") for i in range(2)]
        tower = bank("tower")

        ids_in = sem("ids_in")
        w0_in = sem("w0_in")
        sel_in = sem("sel_in")
        w1_in = sem("w1_in")
        tower_in = sem("tower_in")
        ready = sem("ready")
        zeroed = sem("zeroed")
        rows_ready = sem("rows_ready")
        unit_in = [sem(f"unit_in{i}") for i in range(2)]
        rest_step = sem("rest_step")
        parts_ready = sem("parts_ready")
        ring_full = sem("ring_full")
        ring_drained = sem("ring_drained")
        copied = sem("copied")
        first_ready = sem("first_ready")
        prod_ready = sem("prod_ready")
        hi_ready = sem("hi_ready")
        lo_ready = sem("lo_ready")
        squared = sem("squared")
        square_hi = sem("square_hi")
        square_ready = sem("square_ready")
        tile_used = sem("tile_used")
        square_used = sem("square_used")
        sums_stored = sem("sums_stored")
        turn_full = sem("turn_full")
        turn_drained = sem("turn_drained")
        diag_in = [sem(f"diag_in{i}") for i in range(2)]
        tower_full = sem("tower_full")
        tower_drained = sem("tower_drained")
        stored = sem("stored")

        ring_order = [("field", 0, 0), ("field", 0, 1)]
        for k in range(1, BLOCKS + 1):
            for s in range(SUBS):
                ring_order.append(("dot", k - 1, s))
                if s == 2 and k % 2 and k < BLOCKS - 1:
                    ring_order += [("field", k // 2 + 1, 0), ("field", k // 2 + 1, 1)]
        ring_no = {what: n for n, what in enumerate(ring_order)}
        turn_order = [("dense", 0), ("columns", 0)]
        for k in range(1, BLOCKS + 1):
            turn_order.append(("x1", k - 1))
            if k % 2 and k < BLOCKS - 1:
                turn_order.append(("columns", k // 2 + 1))
        turn_no = {what: n for n, what in enumerate(turn_order)}
        NMLP = 4

        block = ctx.enter_context(nc.Block())

        @block.sync
        def _(sp):
            for f, n in ((0, HALF), (1, FIELDS - HALF)):
                sp.dma_start(ids_sb[64 * f:64 * f + 64, :, 0:n],
                             ids.rearrange("(u b) i -> b u i", b=UNIT)[:, :, HALF * f:HALF * f + n]).then_inc(ids_in, 16)
            sp.dma_start(off_sb[:], offsets).then_inc(ids_in, 16)
            sp.dma_start(sel_f[:], sel).then_inc(sel_in, 16)
            sp.dma_start(back_f[:], back).then_inc(sel_in, 16)
            sp.dma_start(ident_f[:], ident).then_inc(sel_in, 16)
            sp.dma_start(w0a[:], w0_ij).then_inc(w0_in, 16)
            sp.dma_start(w0b[:], w0_ji).then_inc(w0_in, 16)
            sp.dma_start(dense_sb[:], dense.rearrange("(g b) d -> b g d", b=GROUP)).then_inc(tower_in, 16)
            sp.dma_start(wt1_sb[:], wt1[0:2 * P, :].rearrange("(k p) n -> p k n", p=P)).then_inc(tower_in, 16)
            sp.dma_start(wtd_sb[:], wt1[2 * P:2 * P + DIM, :]).then_inc(tower_in, 16)
            sp.dma_start(wt2_sb[:], wt2.rearrange("(k p) n -> p k n", p=P)).then_inc(tower_in, 16)
            sp.dma_start(wt3_sb[:], wt3).then_inc(tower_in, 16)
            sp.dma_start(bt1_sb[:], bt1).then_inc(tower_in, 16)
            sp.dma_start(bt2_sb[:], bt2).then_inc(tower_in, 16)
            sp.dma_start(w1_sb[:], w1.rearrange("(i j) h -> j i h", i=FIELDS)).then_inc(w1_in, 16)
            sp.wait_ge(zeroed, 3)
            for u in range(UNITS):
                sp.wait_ge(turn_drained, turn_no["columns", u] + 1)
                if u >= 2:
                    sp.wait_ge(ring_full, ring_no["dot", 2 * (u - 2) + 1, SUBS - 1] + 1)
                for b in range(SUB):
                    sp.dma_start(diag[DIM * b:DIM * b + DIM, u % 2, :, WIDE * b:WIDE * b + WIDE],
                                 columns[DIM * b:DIM * b + DIM, u % 2, :, :]).then_inc(diag_in[u % 2], 16)
            sp.wait_ge(tower_drained, NMLP * GROUPS)
            sp.dma_start(out.rearrange("b o -> o b"), y[:]).then_inc(stored, 16)
            sp.wait_ge(stored, 16)

        @block.gpsimd
        def _(pool):
            pool.memset(gathered[64:P, :, HALF - 1, :], 0.0).then_inc(zeroed, 1)
            pool.wait_ge(zeroed, 1)
            pool.memset(columns[:, :, :, FIELDS:WIDE], 1.0).then_inc(zeroed, 1)
            pool.wait_ge(zeroed, 2)
            pool.memset(diag[:], 0.0).then_inc(zeroed, 1)
            pool.wait_ge(rows_ready, 2)
            for u in range(UNITS):
                if u >= 2:
                    pool.wait_ge(parts_ready, u - 1)
                for q in range(HALF):
                    n = P if HALF + q < FIELDS else UNIT
                    pool.indirect_dma_start(
                        gathered[0:n, u % 2, q, :], None, table,
                        bass.IndirectOffsetOnAxis(ap=rows[0:n, u, q:q + 1], axis=0)).then_inc(unit_in[u % 2], 16)

        @block.vector
        def _(dve):
            nc.vector.memset(ids_sb[64:P, :, HALF - 1:HALF], 0).then_inc(rows_ready, 1)
            dve.wait_ge(rows_ready, 1)
            dve.wait_ge(ids_in, 48)
            nc.vector.tensor_tensor(rows[:], ids_sb[:], off_sb[:].unsqueeze(1).broadcast_to([P, UNITS, HALF]),
                                    ALU.add).then_inc(rows_ready, 1)
            nc.vector.memset(parts[:, :, :, 3 * HALF:64], 0.0).then_inc(ready, 1)
            dve.wait_ge(sel_in, 48)
            nc.vector.tensor_copy(sel_sb[:], sel_f[:]).then_inc(ready, 1)
            nc.vector.tensor_copy(back_sb[:], back_f[:]).then_inc(ready, 1)
            nc.vector.tensor_copy(ident_b[:], ident_f[:]).then_inc(ready, 1)
            dve.wait_ge(w0_in, 32)
            nc.vector.tensor_tensor(w0s[:], w0a[:], w0b[:], ALU.add).then_inc(ready, 1)
            dve.wait_ge(ready, 5)
            nc.vector.tensor_copy(w0_hi[:], w0s[:]).then_inc(ready, 1)
            dve.wait_ge(ready, 6)
            nc.vector.tensor_tensor(w0_lo[:], w0s[:, 0:TILES, :], w0_hi[:, 0:TILES, :], ALU.subtract).then_inc(ready, 1)
            for quadrant in (1, 3):
                q0 = QUAD * quadrant
                nc.vector.tensor_tensor(w0_hi[q0:q0 + QUAD, TILES, :], w0s[q0:q0 + QUAD, TILES, :],
                                        w0_hi[q0:q0 + QUAD, TILES, :], ALU.subtract).then_inc(ready, 1)

            def split(u, step):
                g = gathered[:, u % 2, :, :].rearrange("p q d -> p d q")
                r = rest[:].rearrange("p q d -> p d q")
                high, middle, low = (parts[:, u % 2, :, HALF * n:HALF * n + HALF] for n in range(3))
                if step == 0:
                    dve.wait_ge(unit_in[u % 2], 16 * HALF * (u // 2 + 1))
                    if u == 0:
                        dve.wait_ge(zeroed, 1)
                    if u >= 2:
                        dve.wait_ge(ring_full, ring_no["field", u - 2, 1] + 1)
                    nc.vector.tensor_copy(high, g).then_inc(rest_step, 1)
                if step == 1:
                    dve.wait_ge(rest_step, 3 * u + 1)
                    nc.vector.tensor_tensor(r, g, high, ALU.subtract).then_inc(rest_step, 1)
                if step == 2:
                    dve.wait_ge(rest_step, 3 * u + 2)
                    nc.vector.tensor_copy(middle, r).then_inc(rest_step, 1)
                if step == 3:
                    dve.wait_ge(rest_step, 3 * u + 3)
                    nc.vector.tensor_tensor(low, r, middle, ALU.subtract).then_inc(parts_ready, 1)

            def product(m):
                k, t = divmod(m, TILES)
                dve.wait_ge(first_ready, k + 1)
                dve.wait_ge(copied, (TILES + 2) * k + 1 + t + 1)
                if m >= NPROD:
                    dve.wait_ge(lo_ready, m - NPROD + 1)
                nc.vector.tensor_tensor(prod[:, m % NPROD, :], first[:, k % 2, :],
                                        copies[((TILES + 2) * k + 1 + t) % 3][:], ALU.mult).then_inc(prod_ready, 1)

            def low(m):
                dve.wait_ge(hi_ready, m + 1)
                if m >= NPART:
                    dve.wait_ge(tile_used, m - NPART + 1)
                nc.vector.tensor_tensor(prod_lo[:, m % NPART, :], prod[:, m % NPROD, :],
                                        prod_hi[:, m % NPART, :], ALU.subtract).then_inc(lo_ready, 1)

            def square_low(k):
                dve.wait_ge(square_hi, k + 1)
                half = square_parts[64:P, k % 2, :]
                nc.vector.tensor_tensor(half, square[64:P, k % 2, :], half, ALU.subtract).then_inc(square_ready, 1)

            for step in range(4):
                split(0, step)
            for k in range(BLOCKS):
                for t in range(TILES):
                    m = TILES * k + t
                    if m and t == 0:
                        low(m - 1)
                    product(m)
                    if t:
                        low(m - 1)
                    if t == 0 and k:
                        square_low(k - 1)
                    if k % 2 and k < BLOCKS - 1 and t < 4:
                        split(k // 2 + 1, t)
            low(TILES * BLOCKS - 1)
            square_low(BLOCKS - 1)

        @block.scalar
        def _(act):
            def store_field(u, half):
                n = ring_no["field", u, half]
                act.wait_ge(ring_full, n + 1)
                p0 = 64 * half
                if u >= 2 and half == 0:
                    act.wait_ge(copied, (TILES + 2) * 2 * (u - 1))
                src = ring[n % 2][:].bitcast(BF16)[p0:p0 + 64, :].rearrange("p (d b) -> p b d", d=DIM)
                nc.scalar.copy(turned[p0:p0 + 64, u % 2, :].rearrange("p (b d) -> p b d", d=DIM), src)\
                    .then_inc(ring_drained, 1)

            def store_columns(u):
                act.wait_ge(turn_full, turn_no["columns", u] + 1)
                if u == 0:
                    act.wait_ge(zeroed, 2)
                if u >= 2:
                    act.wait_ge(diag_in[u % 2], 16 * SUB * (u // 2))
                nc.scalar.copy(columns[:, u % 2, :, 0:FIELDS],
                               turn[:, 0:UNIT // SUB * WIDE].rearrange("p (s i) -> p s i", i=WIDE)[:, :, 0:FIELDS])\
                    .then_inc(turn_drained, 1)

            def store_first(k):
                n = (TILES + 2) * k
                act.wait_ge(copied, n + 1)
                if k >= 2:
                    act.wait_ge(prod_ready, TILES * (k - 1))
                nc.scalar.copy(first[:, k % 2, :], copies[n % 3][:]).then_inc(first_ready, 1)

            def high(m):
                act.wait_ge(prod_ready, m + 1)
                if m >= NPART:
                    act.wait_ge(tile_used, m - NPART + 1)
                    act.wait_ge(lo_ready, m - NPART + 1)
                nc.scalar.copy(prod_hi[:, m % NPART, :], prod[:, m % NPROD, :]).then_inc(hi_ready, 1)

            def square_both(k):
                n = (TILES + 2) * k + TILES + 1
                act.wait_ge(copied, n + 1)
                if k >= 2:
                    act.wait_ge(square_ready, k - 1)
                    act.wait_ge(square_used, k - 1)
                nc.scalar.activation(square[:, k % 2, :], copies[n % 3][:], ACT.Square).then_inc(squared, 1)
                act.wait_ge(squared, k + 1)
                nc.scalar.copy(square_parts[:, k % 2, :], square[:, k % 2, :]).then_inc(square_hi, 1)

            def store_x1(k):
                act.wait_ge(square_used, k + 1)
                if k:
                    act.wait_ge(turn_full, turn_no["x1", k - 1] + 1)
                nc.scalar.copy(x1[:], sums[:]).then_inc(sums_stored, 1)

            def store_turned(k):
                act.wait_ge(turn_full, turn_no["x1", k] + 1)
                if k >= 2:
                    act.wait_ge(ring_full, ring_no["dot", k - 2, SUBS - 1] + 1)
                nc.scalar.copy(x1_turned[:, k % 2, :, :], turn[:].rearrange("p (s h) -> p s h", h=P))\
                    .then_inc(turn_drained, 1)

            def store_dots(k, s):
                n = ring_no["dot", k, s]
                g, at = divmod(k * BLOCK + s * SUB, GROUP)
                act.wait_ge(ring_full, n + 1)
                if g >= 2 and at == 0:
                    act.wait_ge(tower_full, NMLP * (g - 2) + 2)
                nc.scalar.copy(dots[:, g % 2, :, at:at + SUB].rearrange("p i b -> p b i"),
                               ring[n % 2][:, 0:SUB * WIDE].rearrange("p (b i) -> p b i", i=WIDE))\
                    .then_inc(ring_drained, 1)

            def tower_step(g, step):
                act.wait_ge(tower_full, NMLP * g + step + 1)
                if step == 0:
                    last = nc.scalar.copy(z2[:], tower[:, 0:GROUP])
                if step == 1:
                    for n in range(H1 // P):
                        last = nc.scalar.activation(h1[:, n, :], tower[:, GROUP * n:GROUP * n + GROUP], ACT.Relu,
                                                    bias=bt1_sb[:, n:n + 1])
                if step == 2:
                    for n in range(H2 // P):
                        last = nc.scalar.activation(h2[:, n, :], tower[:, GROUP * n:GROUP * n + GROUP], ACT.Relu,
                                                    bias=bt2_sb[:, n:n + 1])
                if step == 3:
                    last = nc.scalar.copy(y[:, GROUP * g:GROUP * g + GROUP], tower[0:1, 0:GROUP])
                last.then_inc(tower_drained, 1)

            act.wait_ge(turn_full, 1)
            nc.scalar.copy(dense_t[:], turn[0:DIM, :]).then_inc(turn_drained, 1)
            store_field(0, 0)
            store_field(0, 1)
            store_first(0)
            store_columns(0)
            for k in range(BLOCKS):
                g, kk = divmod(k, GROUP // BLOCK)
                for t in range(TILES + 1):
                    if t == 0 and k:
                        store_x1(k - 1)
                    if t < TILES:
                        high(TILES * k + t)
                    else:
                        square_both(k)
                    if k and t == 2:
                        store_turned(k - 1)
                    if k and t >= 3:
                        store_dots(k - 1, t - 3)
                        if t == 5 and k % 2 and k < BLOCKS - 1:
                            store_field(k // 2 + 1, 0)
                            store_field(k // 2 + 1, 1)
                    if g and kk == 3 and t in (0, 2, 5):
                        tower_step(g - 1, (0, 2, 5).index(t))
                if k < BLOCKS - 1:
                    store_first(k + 1)
                if k % 2 and k < BLOCKS - 1:
                    store_columns(k // 2 + 1)
                if g and kk == 3:
                    tower_step(g - 1, 3)
            store_x1(BLOCKS - 1)
            store_turned(BLOCKS - 1)
            for s in range(SUBS):
                store_dots(BLOCKS - 1, s)
            for step in range(NMLP):
                tower_step(GROUPS - 1, step)

        @block.tensor
        def _(pe):
            def free_ring(n):
                if n >= 2:
                    pe.wait_ge(ring_drained, n - 1)

            def free_turn(n):
                if n:
                    pe.wait_ge(turn_drained, n)

            def turn_dense():
                pe.wait_ge(tower_in, 16 * 7)
                pe.wait_ge(ready, 4)
                for g in range(GROUPS):
                    mm = pe.transpose(turn[0:DIM, GROUP * g:GROUP * g + GROUP], dense_sb[:, g, :], ident_f[:])
                mm.then_inc(turn_full, 1)

            def turn_fields(u, half):
                n = ring_no["field", u, half]
                pe.wait_ge(parts_ready, u + 1)
                free_ring(n)
                p0 = 64 * half
                to = ring[n % 2][:].bitcast(BF16)
                for d in range(DIM):
                    mm = pe.transpose(to[p0:p0 + 64, UNIT * d:UNIT * d + UNIT], parts[p0:p0 + 64, u % 2, d, :],
                                      ident_b[p0:p0 + 64, p0:p0 + 64])
                mm.then_inc(ring_full, 1)

            def fields_by_column(u):
                pe.wait_ge(ring_drained, ring_no["field", u, 1] + 1)
                free_turn(turn_no["columns", u])
                for s in range(UNIT // SUB):
                    mm = pe.matmul(turn[:, WIDE * s:WIDE * s + WIDE], turned[:, u % 2, P * s:P * s + P], back_sb[:],
                                   start=True, stop=True)
                mm.then_inc(turn_full, 1)

            def copy_rows(n):
                if n >= (TILES + 2) * BLOCKS:
                    return
                k, e = divmod(n, TILES + 2)
                if e == 0:
                    pe.wait_ge(ring_drained, ring_no["field", k // 2, 1] + 1)
                if n >= 3:
                    before, was = divmod(n - 3, TILES + 2)
                    if was == 0:
                        pe.wait_ge(first_ready, before + 1)
                    elif was <= TILES:
                        pe.wait_ge(prod_ready, TILES * before + was)
                    else:
                        pe.wait_ge(squared, before + 1)
                at = COLS * (k % 2)
                pe.matmul(copies[n % 3][:], sel_sb[:, e, :], turned[:, k // 2 % 2, at:at + COLS],
                          start=True, stop=True).then_inc(copied, 1)

            def add_tile(k, t):
                m = TILES * k + t
                if t == 0 and k:
                    pe.wait_ge(sums_stored, k)
                pe.wait_ge(lo_ready, m + 1)
                hi, lo = prod_hi[:, m % NPART, :], prod_lo[:, m % NPART, :]
                pe.matmul(sums[:], w0_hi[:, t, :], hi, start=(t == 0), stop=False)
                pe.matmul(sums[:], w0_hi[:, t, :], lo, start=False, stop=False)
                pe.matmul(sums[:], w0_lo[:, t, :], hi, start=False, stop=False).then_inc(tile_used, 1)

            def add_squares(k):
                pe.wait_ge(square_ready, k + 1)
                pe.matmul(sums[:], w0_hi[:, TILES, :], square_parts[:, k % 2, :], start=False, stop=True)\
                    .then_inc(square_used, 1)

            def turn_x1(k):
                pe.wait_ge(sums_stored, k + 1)
                free_turn(turn_no["x1", k])
                for s in range(SUBS):
                    mm = pe.transpose(turn[:, P * s:P * s + P], x1[:, P * s:P * s + P], ident_f[:])
                mm.then_inc(turn_full, 1)

            def dot(k, s):
                n = ring_no["dot", k, s]
                u = k // 2
                pe.wait_ge(turn_drained, turn_no["x1", k] + 1)
                pe.wait_ge(diag_in[u % 2], 16 * SUB * (u // 2 + 1))
                free_ring(n)
                pe.matmul(ring[n % 2][:, 0:SUB * WIDE], x1_turned[:, k % 2, s, :], diag[:, u % 2, SUBS * (k % 2) + s, :],
                          start=True, stop=True).then_inc(ring_full, 1)

            def second_layer(g, i0, i1):
                for i in range(i0, min(i1, FIELDS)):
                    if i == 0:
                        pe.wait_ge(w1_in, 16)
                        if g:
                            pe.wait_ge(tower_drained, NMLP * g)
                        pe.wait_ge(ring_drained, ring_no["dot", 4 * g + 3, SUBS - 1] + 1)
                    mm = pe.matmul(tower[:, 0:GROUP], w1_sb[:, i, :], dots[:, g % 2, i, :],
                                   start=(i == 0), stop=(i == FIELDS - 1))
                    if i == FIELDS - 1:
                        mm.then_inc(tower_full, 1)

            def tower_step(g, step):
                pe.wait_ge(tower_drained, NMLP * g + step)
                if step == 1:
                    if g == 0:
                        pe.wait_ge(turn_drained, turn_no["dense", 0] + 1)
                    for n in range(H1 // P):
                        to, cols = tower[:, GROUP * n:GROUP * n + GROUP], slice(P * n, P * n + P)
                        pe.matmul(to, wt1_sb[:, 0, cols], dots[:, g % 2, FIELDS, :], start=True, stop=False)
                        pe.matmul(to, wt1_sb[:, 1, cols], z2[:], start=False, stop=False)
                        mm = pe.matmul(to, wtd_sb[:, cols], dense_t[:, GROUP * g:GROUP * g + GROUP],
                                       start=False, stop=True)
                if step == 2:
                    for n in range(H2 // P):
                        for j in range(H1 // P):
                            mm = pe.matmul(tower[:, GROUP * n:GROUP * n + GROUP], wt2_sb[:, j, P * n:P * n + P],
                                           h1[:, j, :], start=(j == 0), stop=(j == H1 // P - 1))
                if step == 3:
                    for j in range(H2 // P):
                        mm = pe.matmul(tower[0:1, 0:GROUP], wt3_sb[:, j:j + 1], h2[:, j, :],
                                       start=(j == 0), stop=(j == H2 // P - 1))
                mm.then_inc(tower_full, 1)

            turn_dense()
            turn_fields(0, 0)
            turn_fields(0, 1)
            for n in range(3):
                copy_rows(n)
            fields_by_column(0)
            pe.wait_ge(ready, 9)
            for k in range(BLOCKS):
                g, kk = divmod(k, GROUP // BLOCK)
                for t in range(TILES + 1):
                    copy_rows((TILES + 2) * k + t + 3)
                    if t == TILES:
                        copy_rows((TILES + 2) * k + t + 4)
                    if t < TILES:
                        add_tile(k, t)
                    else:
                        add_squares(k)
                    if k and t == 1:
                        turn_x1(k - 1)
                    if k and 2 <= t < 2 + SUBS:
                        dot(k - 1, t - 2)
                        if t == 4 and k % 2 and k < BLOCKS - 1:
                            turn_fields(k // 2 + 1, 0)
                            turn_fields(k // 2 + 1, 1)
                            fields_by_column(k // 2 + 1)
                    if g and kk in (1, 2):
                        at = 3 * ((TILES + 1) * (kk - 1) + t)
                        second_layer(g - 1, at, at + 3)
                    if g and kk == 3 and t in (1, 4, 6):
                        tower_step(g - 1, (1, 4, 6).index(t) + 1)
            last = BLOCKS - 1
            turn_x1(last)
            for s in range(SUBS):
                dot(last, s)
            second_layer(GROUPS - 1, 0, FIELDS)
            for step in (1, 2, 3):
                tower_step(GROUPS - 1, step)


def kernel(dense_ctx, ids, W_top1, b_top1, W_top2, b_top2, W_top3, L0_rec_W0, L0_rec_W1, **tables):
    import concourse.bacc as bacc
    from concourse.bass_utils import run_bass_kernel_spmd

    tabs = [np.asarray(tables[f"tbl_{i}"]) for i in range(FIELDS)]
    starts = np.cumsum([0] + [t.shape[0] for t in tabs])[:FIELDS]
    offsets = np.zeros((P, HALF), np.int32)
    for i in range(FIELDS):
        offsets[64 * (i // HALF):64 * (i // HALF) + 64, i % HALF] = starts[i]
    sel, back = selections()
    ij, ji = pair_rows()
    w0 = np.concatenate([np.asarray(L0_rec_W0)[0], np.zeros((1, P), np.float32)])
    arrays = {
        "table": np.concatenate(tabs),
        "ids": np.asarray(ids),
        "offsets": offsets,
        "w0_ij": np.ascontiguousarray(w0[ij.T]),
        "w0_ji": np.ascontiguousarray(w0[ji.T]),
        "w1": np.asarray(L0_rec_W1)[0],
        "sel": sel,
        "back": back,
        "ident": np.eye(P, dtype=np.float32),
        "dense": np.asarray(dense_ctx),
        "wt1": np.asarray(W_top1),
        "bt1": np.ascontiguousarray(np.asarray(b_top1).reshape(-1, P).T),
        "wt2": np.asarray(W_top2),
        "bt2": np.ascontiguousarray(np.asarray(b_top2).reshape(-1, P).T),
        "wt3": np.ascontiguousarray(np.asarray(W_top3).reshape(-1, P).T),
    }
    nc = bacc.Bacc("TRN2", target_bir_lowering=False, num_devices=1)
    args = {n: nc.dram_tensor(n, a.shape, mybir.dt.from_np(a.dtype), kind="ExternalInput").ap() for n, a in arrays.items()}
    out = nc.dram_tensor("out", (BATCH, 1), F32, kind="ExternalOutput").ap()
    build(nc, **args, out=out)
    return run_bass_kernel_spmd(nc, [arrays], core_ids=[0]).results[0]["out"]
```

```python
from contextlib import ExitStack

import numpy as np

import concourse.bass as bass
from concourse import mybir

ALU = mybir.AluOpType
ACT = mybir.ActivationFunctionType
F32 = mybir.dt.float32
F32R = mybir.dt.float32r
BF16 = mybir.dt.bfloat16
I32 = mybir.dt.int32

P = 128
FIELDS = 39
DIM = 16
BATCH = 512
HALF = 20
UNIT = 64
UNITS = BATCH // UNIT
BLOCK = 32
BLOCKS = BATCH // BLOCK
GROUP = 128
GROUPS = BATCH // GROUP
COLS = BLOCK * DIM
SUB = P // DIM
SUBS = BLOCK // SUB
WIDE = FIELDS + 1
TILES = 6
LEFT = FIELDS * (FIELDS + 1) // 2 - TILES * P
QUAD = 32
H1, H2 = 512, 256


def first_of_pair():
    return [p % FIELDS for p in range(P)]


def pair_tiles():
    first = first_of_pair()
    room = {i: TILES * first.count(i) for i in range(FIELDS)}
    partners = {i: [i] if i >= LEFT else [] for i in range(FIELDS)}
    need = {i: room[i] - len(partners[i]) for i in range(FIELDS)}
    open_fields = list(range(FIELDS))
    while open_fields:
        open_fields.sort(key=lambda i: (need[i], i))
        v = open_fields.pop(0)
        wins = need[v]
        for n, w in enumerate(open_fields):
            if n < wins:
                partners[v].append(w)
            else:
                partners[w].append(v)
                need[w] -= 1
        assert 0 <= wins <= len(open_fields)
    assert all(len(partners[i]) == room[i] for i in range(FIELDS))
    tiles = []
    for _ in range(TILES):
        tiles.append([partners[i].pop() for i in first])
    return tiles


def part_row(field, part):
    return 64 * (field // HALF) + part * HALF + field % HALF


def selections():
    sel = np.zeros((P, TILES + 2, P), np.float32)
    back = np.zeros((P, WIDE), np.float32)
    tiles = [first_of_pair(), *pair_tiles()]
    for n, fields in enumerate(tiles):
        for p, i in enumerate(fields):
            for part in range(3):
                sel[part_row(i, part), n, p] = 1
    for i in range(LEFT):
        for quadrant in range(4):
            for part in range(3):
                sel[part_row(i, part), TILES + 1, QUAD * quadrant + i] = 1
    for i in range(FIELDS):
        for part in range(3):
            back[part_row(i, part), i] = 1
    return sel, back


def pair_rows():
    first, none = first_of_pair(), FIELDS * FIELDS
    ij = np.full((TILES + 1, P), none)
    ji = np.full((TILES + 1, P), none)
    for t, second in enumerate(pair_tiles()):
        for p, (i, j) in enumerate(zip(first, second)):
            ij[t, p] = i * FIELDS + j
            if i != j:
                ji[t, p] = j * FIELDS + i
    for quadrant in range(4):
        for i in range(LEFT):
            ij[TILES, QUAD * quadrant + i] = i * FIELDS + i
    return ij, ji


def build(nc, table, ids, offsets, w0_ij, w0_ji, w1, sel, back, ident, dense, wt1, bt1, wt2, bt2, wt3, out):
    ctx = ExitStack()
    with ctx:
        def sb(name, shape, dt=F32):
            return ctx.enter_context(nc.sbuf_tensor(name, shape, dt))

        def bank(name, shape=(P, COLS), dt=F32):
            return ctx.enter_context(nc.psum_tensor(name, list(shape), dt))

        def sem(name):
            return ctx.enter_context(nc.semaphore(name))

        NPROD, NPART = 4, 6
        ids_sb = sb("ids_sb", [P, UNITS, HALF], I32)
        off_sb = sb("off_sb", [P, HALF], I32)
        rows = sb("rows", [P, UNITS, HALF], I32)
        gathered = sb("gathered", [P, 2, HALF, DIM])
        rest = sb("rest", [P, HALF, DIM])
        parts = sb("parts", [P, 2, DIM, 64], BF16)
        turned = sb("turned", [P, 2, UNIT * DIM], BF16)
        sel_f = sb("sel_f", [P, TILES + 2, P])
        sel_sb = sb("sel_sb", [P, TILES + 2, P], BF16)
        back_f = sb("back_f", [P, WIDE])
        back_sb = sb("back_sb", [P, WIDE], BF16)
        ident_f = sb("ident_f", [P, P])
        ident_b = sb("ident_b", [P, P], BF16)
        w0a = sb("w0a", [P, TILES + 1, P])
        w0b = sb("w0b", [P, TILES + 1, P])
        w0_hi = sb("w0_hi", [P, TILES + 1, P], F32R)
        w0_lo = sb("w0_lo", [P, TILES, P], F32R)
        first = sb("first", [P, 2, COLS])
        prod = sb("prod", [P, NPROD, COLS])
        prod_hi = sb("prod_hi", [P, NPART, COLS], F32R)
        prod_lo = sb("prod_lo", [P, NPART, COLS], F32R)
        square = sb("square", [P, 2, COLS])
        square_parts = sb("square_parts", [P, 2, COLS], F32R)
        x1 = sb("x1", [P, COLS])
        turned_hi = sb("turned_hi", [P, 2, SUBS, P], F32R)
        turned_lo = sb("turned_lo", [P, 2, SUBS, P], F32R)
        columns = sb("columns", [P, 2, UNIT // SUB, 2, WIDE], F32R)
        diag = sb("diag", [P, 2, SUBS, 2, SUB * WIDE], F32R)
        dots = sb("dots", [P, 2, WIDE, GROUP])
        w1_sb = sb("w1_sb", [P, FIELDS, P])
        dense_sb = sb("dense_sb", [P, GROUPS, DIM])
        dense_t = sb("dense_t", [DIM, BATCH])
        wt1_sb = sb("wt1_sb", [P, 2, H1])
        wtd_sb = sb("wtd_sb", [DIM, H1])
        wt2_sb = sb("wt2_sb", [P, H1 // P, H2])
        wt3_sb = sb("wt3_sb", [P, H2 // P])
        bt1_sb = sb("bt1_sb", [P, H1 // P])
        bt2_sb = sb("bt2_sb", [P, H2 // P])
        z2 = sb("z2", [P, GROUP])
        h1 = sb("h1", [P, H1 // P, GROUP])
        h2 = sb("h2", [P, H2 // P, GROUP])
        y = sb("y", [1, BATCH])

        copies = [bank(f"copies{i}") for i in range(3)]
        sums = [bank(f"sums{i}") for i in range(2)]
        ring = [bank(f"ring{i}") for i in range(2)]
        tower = bank("tower")

        ids_in = sem("ids_in")
        w0_in = sem("w0_in")
        sel_in = sem("sel_in")
        w1_in = sem("w1_in")
        ring_low = sem("ring_low")
        tower_in = sem("tower_in")
        ready = sem("ready")
        zeroed = sem("zeroed")
        rows_ready = sem("rows_ready")
        unit_in = [sem(f"unit_in{i}") for i in range(2)]
        rest_step = sem("rest_step")
        parts_ready = sem("parts_ready")
        ring_full = sem("ring_full")
        ring_drained = sem("ring_drained")
        copied = sem("copied")
        first_ready = sem("first_ready")
        prod_ready = sem("prod_ready")
        hi_ready = sem("hi_ready")
        lo_ready = sem("lo_ready")
        squared = sem("squared")
        square_hi = sem("square_hi")
        square_ready = sem("square_ready")
        tile_used = sem("tile_used")
        square_used = sem("square_used")
        sums_stored = sem("sums_stored")
        diag_in = [sem(f"diag_in{i}") for i in range(2)]
        tower_full = sem("tower_full")
        tower_drained = sem("tower_drained")
        stored = sem("stored")

        steps = [0, 1, 2, 3, "S", 4, 5]
        copy_order = [("first", 0), ("second", 0, 0), ("second", 0, 1), ("second", 0, 2)]
        copies_before = {}
        for k in range(BLOCKS):
            for step, new in ((0, [("second", k, 3)]),
                              (1, [("squares", k), ("second", k, 4)]),
                              (2, [("first", k + 1), ("second", k, 5)]),
                              (3, [("second", k + 1, 0)]),
                              (4, [("second", k + 1, 1)]),
                              (5, [("second", k + 1, 2)])):
                copies_before[k, step] = [x for x in new if x[1] < BLOCKS]
                copy_order += copies_before[k, step]
        copy_no = {what: n for n, what in enumerate(copy_order)}
        ring_order = [("dense", 0), ("field", 0, 0), ("field", 0, 1), ("columns", 0)]
        ring_after = {}
        for k in range(BLOCKS + 1):
            for step, new in ((0, [("field", k // 2 + 1, 0), ("field", k // 2 + 1, 1)]),
                              (1, [("x1", k - 1)]),
                              (3, [("dot", k - 1, 0)]),
                              ("S", [("dot", k - 1, 1)]),
                              (4, [("dot", k - 1, 2), ("columns", k // 2 + 1)]),
                              (5, [("dot", k - 1, 3)])):
                ring_after[k, step] = [x for x in new if (k > 0 if x[0] in ("x1", "dot") else k % 2 and k < BLOCKS - 1)]
                ring_order += ring_after[k, step]
        ring_no = {what: n for n, what in enumerate(ring_order)}
        low_no = {what: n for n, what in enumerate(x for x in ring_order if x[0] in ("columns", "x1"))}
        NMLP = 4
        tower_fills, tower_stores = {}, {}
        for g in range(GROUPS - 1):
            k = 4 * (g + 1)
            for n, (dk, step) in enumerate(((2, 4), (3, 1), (3, 4), (4, 1))):
                tower_fills[k + dk, step] = (g, n)
            for n, (dk, step) in enumerate(((3, 0), (3, 2), (3, 5), (4, 2))):
                tower_stores[k + dk, step] = (g, n)

        def by_sub(of):
            return of[:, 0:UNIT // SUB * WIDE].rearrange("p (s i) -> p s i", i=WIDE)

        block = ctx.enter_context(nc.Block())

        @block.sync
        def _(sp):
            for f, n in ((0, HALF), (1, FIELDS - HALF)):
                sp.dma_start(ids_sb[64 * f:64 * f + 64, :, 0:n],
                             ids.rearrange("(u b) i -> b u i", b=UNIT)[:, :, HALF * f:HALF * f + n]).then_inc(ids_in, 16)
            sp.dma_start(off_sb[:], offsets).then_inc(ids_in, 16)
            sp.dma_start(sel_f[:], sel).then_inc(sel_in, 16)
            sp.dma_start(back_f[:], back).then_inc(sel_in, 16)
            sp.dma_start(ident_f[:], ident).then_inc(sel_in, 16)
            sp.dma_start(w0a[:], w0_ij).then_inc(w0_in, 16)
            sp.dma_start(w0b[:], w0_ji).then_inc(w0_in, 16)
            sp.dma_start(dense_sb[:], dense.rearrange("(g b) d -> b g d", b=GROUP)).then_inc(tower_in, 16)
            sp.dma_start(wt1_sb[:], wt1[0:2 * P, :].rearrange("(k p) n -> p k n", p=P)).then_inc(tower_in, 16)
            sp.dma_start(wtd_sb[:], wt1[2 * P:2 * P + DIM, :]).then_inc(tower_in, 16)
            sp.dma_start(wt2_sb[:], wt2.rearrange("(k p) n -> p k n", p=P)).then_inc(tower_in, 16)
            sp.dma_start(wt3_sb[:], wt3).then_inc(tower_in, 16)
            sp.dma_start(bt1_sb[:], bt1).then_inc(tower_in, 16)
            sp.dma_start(bt2_sb[:], bt2).then_inc(tower_in, 16)
            sp.dma_start(w1_sb[:], w1.rearrange("(i j) h -> j i h", i=FIELDS)).then_inc(w1_in, 16)
            sp.wait_ge(zeroed, 4)
            for k in range(BLOCKS):
                u, s0 = k // 2, SUBS * (k % 2)
                sp.wait_ge(ring_low, low_no["columns", u] + 1)
                if k >= 2:
                    sp.wait_ge(ring_full, ring_no["dot", k - 2, SUBS - 1] + 1)
                for b in range(SUB):
                    sp.dma_start(diag[DIM * b:DIM * b + DIM, k % 2, :, :, WIDE * b:WIDE * b + WIDE].bitcast(F32),
                                 columns[DIM * b:DIM * b + DIM, u % 2, s0:s0 + SUBS, :, :].bitcast(F32))\
                        .then_inc(diag_in[k % 2], 16)
            sp.wait_ge(tower_drained, NMLP * GROUPS)
            sp.dma_start(out.rearrange("b o -> o b"), y[:]).then_inc(stored, 16)
            sp.wait_ge(stored, 16)

        @block.gpsimd
        def _(pool):
            pool.memset(gathered[64:P, :, HALF - 1, :], 0.0).then_inc(zeroed, 1)
            pool.wait_ge(zeroed, 1)
            pool.memset(columns[:, :, :, 0, FIELDS:WIDE].bitcast(F32), 1.0).then_inc(zeroed, 1)
            pool.wait_ge(zeroed, 2)
            pool.memset(columns[:, :, :, 1, FIELDS:WIDE].bitcast(F32), 0.0).then_inc(zeroed, 1)
            pool.wait_ge(zeroed, 3)
            pool.memset(diag[:].bitcast(F32), 0.0).then_inc(zeroed, 1)
            pool.wait_ge(rows_ready, 2)
            for u in range(UNITS):
                if u >= 2:
                    pool.wait_ge(parts_ready, u - 1)
                for q in range(HALF):
                    n = P if HALF + q < FIELDS else UNIT
                    pool.indirect_dma_start(
                        gathered[0:n, u % 2, q, :], None, table,
                        bass.IndirectOffsetOnAxis(ap=rows[0:n, u, q:q + 1], axis=0)).then_inc(unit_in[u % 2], 16)

        @block.vector
        def _(dve):
            nc.vector.memset(ids_sb[64:P, :, HALF - 1:HALF], 0).then_inc(rows_ready, 1)
            dve.wait_ge(rows_ready, 1)
            dve.wait_ge(ids_in, 48)
            nc.vector.tensor_tensor(rows[:], ids_sb[:], off_sb[:].unsqueeze(1).broadcast_to([P, UNITS, HALF]),
                                    ALU.add).then_inc(rows_ready, 1)
            nc.vector.memset(parts[:, :, :, 3 * HALF:64], 0.0).then_inc(ready, 1)
            dve.wait_ge(sel_in, 48)
            nc.vector.tensor_copy(sel_sb[:], sel_f[:]).then_inc(ready, 1)
            nc.vector.tensor_copy(back_sb[:], back_f[:]).then_inc(ready, 1)
            nc.vector.tensor_copy(ident_b[:], ident_f[:]).then_inc(ready, 1)
            dve.wait_ge(w0_in, 32)
            nc.vector.tensor_tensor(w0a[:], w0a[:], w0b[:], ALU.add).then_inc(ready, 1)
            dve.wait_ge(ready, 5)
            nc.vector.tensor_copy(w0_hi[:], w0a[:]).then_inc(ready, 1)
            dve.wait_ge(ready, 6)
            nc.vector.tensor_tensor(w0_lo[:], w0a[:, 0:TILES, :], w0_hi[:, 0:TILES, :], ALU.subtract).then_inc(ready, 1)
            for quadrant in (1, 3):
                q0 = QUAD * quadrant
                nc.vector.tensor_tensor(w0_hi[q0:q0 + QUAD, TILES, :], w0a[q0:q0 + QUAD, TILES, :],
                                        w0_hi[q0:q0 + QUAD, TILES, :], ALU.subtract).then_inc(ready, 1)

            def split(u, step):
                g = gathered[:, u % 2, :, :].rearrange("p q d -> p d q")
                r = rest[:].rearrange("p q d -> p d q")
                high, middle, low = (parts[:, u % 2, :, HALF * n:HALF * n + HALF] for n in range(3))
                if step == 0:
                    dve.wait_ge(unit_in[u % 2], 16 * HALF * (u // 2 + 1))
                    if u == 0:
                        dve.wait_ge(zeroed, 1)
                    if u >= 2:
                        dve.wait_ge(ring_full, ring_no["field", u - 2, 1] + 1)
                    nc.vector.tensor_copy(high, g).then_inc(rest_step, 1)
                if step == 1:
                    dve.wait_ge(rest_step, 3 * u + 1)
                    nc.vector.tensor_tensor(r, g, high, ALU.subtract).then_inc(rest_step, 1)
                if step == 2:
                    dve.wait_ge(rest_step, 3 * u + 2)
                    nc.vector.tensor_copy(middle, r).then_inc(rest_step, 1)
                if step == 3:
                    dve.wait_ge(rest_step, 3 * u + 3)
                    nc.vector.tensor_tensor(low, r, middle, ALU.subtract).then_inc(parts_ready, 1)

            def product(m):
                k, t = divmod(m, TILES)
                n = copy_no["second", k, t]
                dve.wait_ge(first_ready, k + 1)
                dve.wait_ge(copied, n + 1)
                if m >= NPROD:
                    dve.wait_ge(lo_ready, m - NPROD + 1)
                nc.vector.tensor_tensor(prod[:, m % NPROD, :], first[:, k % 2, :], copies[n % 3][:], ALU.mult)\
                    .then_inc(prod_ready, 1)

            def low(m):
                dve.wait_ge(hi_ready, m + 1)
                if m >= NPART:
                    dve.wait_ge(tile_used, m - NPART + 1)
                nc.vector.tensor_tensor(prod_lo[:, m % NPART, :], prod[:, m % NPROD, :],
                                        prod_hi[:, m % NPART, :], ALU.subtract).then_inc(lo_ready, 1)

            def square_low(k):
                dve.wait_ge(square_hi, k + 1)
                half = square_parts[64:P, k % 2, :]
                nc.vector.tensor_tensor(half, square[64:P, k % 2, :], half, ALU.subtract).then_inc(square_ready, 1)

            def columns_low(u):
                n = ring_no["columns", u]
                dve.wait_ge(ring_drained, n + 1)
                if u >= 2:
                    dve.wait_ge(diag_in[1], 16 * SUB * (u - 1))
                nc.vector.tensor_tensor(columns[:, u % 2, :, 1, 0:FIELDS], by_sub(ring[n % 2])[:, :, 0:FIELDS],
                                        columns[:, u % 2, :, 0, 0:FIELDS], ALU.subtract).then_inc(ring_low, 1)

            def turned_low(k):
                n = ring_no["x1", k]
                dve.wait_ge(ring_drained, n + 1)
                if k >= 2:
                    dve.wait_ge(ring_full, ring_no["dot", k - 2, SUBS - 1] + 1)
                nc.vector.tensor_tensor(turned_lo[:, k % 2, :, :], ring[n % 2][:].rearrange("p (s h) -> p s h", h=P),
                                        turned_hi[:, k % 2, :, :], ALU.subtract).then_inc(ring_low, 1)

            def after(k, step):
                for what in ring_after.get((k, step), []):
                    if what[0] == "columns":
                        columns_low(what[1])
                    if what[0] == "x1":
                        turned_low(what[1])

            for step in range(4):
                split(0, step)
            columns_low(0)
            before = None
            product(0)
            product(1)
            for k in range(BLOCKS):
                for step in steps:
                    if step == "S":
                        square_low(k)
                    else:
                        m = TILES * k + step
                        if m + 2 < TILES * BLOCKS:
                            product(m + 2)
                        low(m)
                        if k % 2 == 0 and k < BLOCKS - 2 and step >= 4:
                            split(k // 2 + 1, 2 * (step - 4))
                            split(k // 2 + 1, 2 * (step - 4) + 1)
                    if before:
                        after(*before)
                    before = (k, step)
            after(*before)
            for step in steps:
                after(BLOCKS, step)

        @block.scalar
        def _(act):
            def store_field(u, half):
                n = ring_no["field", u, half]
                act.wait_ge(ring_full, n + 1)
                p0 = 64 * half
                if u >= 2 and half == 0:
                    act.wait_ge(copied, max(copy_no["second", 2 * u - 3, TILES - 1], copy_no["squares", 2 * u - 3]) + 1)
                    act.wait_ge(ring_full, ring_no["columns", u - 2] + 1)
                src = ring[n % 2][:].bitcast(BF16)[p0:p0 + 64, :].rearrange("p (d b) -> p b d", d=DIM)
                nc.scalar.copy(turned[p0:p0 + 64, u % 2, :].rearrange("p (b d) -> p b d", d=DIM), src)\
                    .then_inc(ring_drained, 1)

            def store_columns(u):
                n = ring_no["columns", u]
                act.wait_ge(ring_full, n + 1)
                if u >= 2:
                    act.wait_ge(diag_in[1], 16 * SUB * (u - 1))
                nc.scalar.copy(columns[:, u % 2, :, 0, 0:FIELDS], by_sub(ring[n % 2])[:, :, 0:FIELDS])\
                    .then_inc(ring_drained, 1)

            def store_first(k):
                n = copy_no["first", k]
                act.wait_ge(copied, n + 1)
                if k >= 2:
                    act.wait_ge(prod_ready, TILES * (k - 1))
                nc.scalar.copy(first[:, k % 2, :], copies[n % 3][:]).then_inc(first_ready, 1)

            def high(m):
                act.wait_ge(prod_ready, m + 1)
                if m >= NPART:
                    act.wait_ge(tile_used, m - NPART + 1)
                    act.wait_ge(lo_ready, m - NPART + 1)
                nc.scalar.copy(prod_hi[:, m % NPART, :], prod[:, m % NPROD, :]).then_inc(hi_ready, 1)

            def square_both(k):
                n = copy_no["squares", k]
                act.wait_ge(copied, n + 1)
                if k >= 2:
                    act.wait_ge(square_ready, k - 1)
                    act.wait_ge(square_used, k - 1)
                nc.scalar.activation(square[:, k % 2, :], copies[n % 3][:], ACT.Square).then_inc(squared, 1)
                act.wait_ge(squared, k + 1)
                nc.scalar.copy(square_parts[:, k % 2, :], square[:, k % 2, :]).then_inc(square_hi, 1)

            def store_x1(k):
                act.wait_ge(tile_used, TILES * (k + 1))
                if k:
                    act.wait_ge(ring_full, ring_no["x1", k - 1] + 1)
                nc.scalar.copy(x1[:], sums[k % 2][:]).then_inc(sums_stored, 1)

            def store_turned(k):
                n = ring_no["x1", k]
                act.wait_ge(ring_full, n + 1)
                if k >= 2:
                    act.wait_ge(ring_full, ring_no["dot", k - 2, SUBS - 1] + 1)
                nc.scalar.copy(turned_hi[:, k % 2, :, :], ring[n % 2][:].rearrange("p (s h) -> p s h", h=P))\
                    .then_inc(ring_drained, 1)

            def store_dots(k, s):
                n = ring_no["dot", k, s]
                g, at = divmod(k * BLOCK + s * SUB, GROUP)
                act.wait_ge(ring_full, n + 1)
                if g >= 2 and at == 0:
                    act.wait_ge(tower_full, NMLP * (g - 2) + 2)
                nc.scalar.copy(dots[:, g % 2, :, at:at + SUB].rearrange("p i b -> p b i"),
                               ring[n % 2][:, 0:SUB * WIDE].rearrange("p (b i) -> p b i", i=WIDE))\
                    .then_inc(ring_drained, 1)

            def tower_step(g, step):
                act.wait_ge(tower_full, NMLP * g + step + 1)
                if step == 0:
                    last = nc.scalar.copy(z2[:], tower[:, 0:GROUP])
                if step == 1:
                    for n in range(H1 // P):
                        last = nc.scalar.activation(h1[:, n, :], tower[:, GROUP * n:GROUP * n + GROUP], ACT.Relu,
                                                    bias=bt1_sb[:, n:n + 1])
                if step == 2:
                    for n in range(H2 // P):
                        last = nc.scalar.activation(h2[:, n, :], tower[:, GROUP * n:GROUP * n + GROUP], ACT.Relu,
                                                    bias=bt2_sb[:, n:n + 1])
                if step == 3:
                    last = nc.scalar.copy(y[:, GROUP * g:GROUP * g + GROUP], tower[0:1, 0:GROUP])
                last.then_inc(tower_drained, 1)

            act.wait_ge(ring_full, 1)
            nc.scalar.copy(dense_t[:], ring[0][0:DIM, :]).then_inc(ring_drained, 1)
            store_field(0, 0)
            store_field(0, 1)
            store_first(0)
            store_columns(0)

            def after(k, step):
                if step == 5 and k < BLOCKS:
                    store_x1(k)
                for what in copies_before.get((k, step), []):
                    if what[0] == "first":
                        store_first(what[1])
                    if what[0] == "squares":
                        square_both(what[1])
                for what in ring_after[k, step] if (k, step) in ring_after else []:
                    {"field": store_field, "columns": store_columns, "x1": store_turned, "dot": store_dots}[what[0]](*what[1:])
                if (k, step) in tower_stores:
                    tower_step(*tower_stores[k, step])

            high(0)
            high(1)
            for k in range(BLOCKS):
                for step in steps:
                    if step != "S" and TILES * k + step + 2 < TILES * BLOCKS:
                        high(TILES * k + step + 2)
                    after(k, step)
            for step in steps:
                after(BLOCKS, step)
            for step in range(NMLP):
                tower_step(GROUPS - 1, step)

        @block.tensor
        def _(pe):
            def free_ring(n):
                if n >= 2:
                    was = ring_order[n - 2]
                    if was in low_no:
                        pe.wait_ge(ring_low, low_no[was] + 1)
                    else:
                        pe.wait_ge(ring_drained, n - 1)

            def turn_dense():
                pe.wait_ge(tower_in, 16 * 7)
                pe.wait_ge(ready, 4)
                for g in range(GROUPS):
                    mm = pe.transpose(ring[0][0:DIM, GROUP * g:GROUP * g + GROUP], dense_sb[:, g, :], ident_f[:])
                mm.then_inc(ring_full, 1)

            def turn_fields(u, half):
                n = ring_no["field", u, half]
                pe.wait_ge(parts_ready, u + 1)
                free_ring(n)
                p0 = 64 * half
                to = ring[n % 2][:].bitcast(BF16)
                for d in range(DIM):
                    mm = pe.transpose(to[p0:p0 + 64, UNIT * d:UNIT * d + UNIT], parts[p0:p0 + 64, u % 2, d, :],
                                      ident_b[p0:p0 + 64, p0:p0 + 64])
                mm.then_inc(ring_full, 1)

            def fields_by_column(u):
                pe.wait_ge(ring_drained, ring_no["field", u, 1] + 1)
                n = ring_no["columns", u]
                free_ring(n)
                for s in range(UNIT // SUB):
                    mm = pe.matmul(ring[n % 2][:, WIDE * s:WIDE * s + WIDE], turned[:, u % 2, P * s:P * s + P], back_sb[:],
                                   start=True, stop=True)
                mm.then_inc(ring_full, 1)

            def copy_rows(what):
                n = copy_no[what]
                kind, k = what[0:2]
                e = {"first": 0, "second": 1 + what[-1], "squares": TILES + 1}[kind]
                if kind == "first":
                    pe.wait_ge(ring_drained, ring_no["field", k // 2, 1] + 1)
                if n >= 3:
                    was = copy_order[n - 3]
                    if was[0] == "first":
                        pe.wait_ge(first_ready, was[1] + 1)
                    elif was[0] == "second":
                        pe.wait_ge(prod_ready, TILES * was[1] + was[2] + 1)
                    else:
                        pe.wait_ge(squared, was[1] + 1)
                at = COLS * (k % 2)
                pe.matmul(copies[n % 3][:], sel_sb[:, e, :], turned[:, k // 2 % 2, at:at + COLS],
                          start=True, stop=True).then_inc(copied, 1)

            def add_tile(k, t):
                m = TILES * k + t
                if t == 0 and k >= 2:
                    pe.wait_ge(sums_stored, k - 1)
                pe.wait_ge(lo_ready, m + 1)
                hi, lo = prod_hi[:, m % NPART, :], prod_lo[:, m % NPART, :]
                to = sums[k % 2][:]
                pe.matmul(to, w0_hi[:, t, :], hi, start=(t == 0), stop=False)
                pe.matmul(to, w0_hi[:, t, :], lo, start=False, stop=False)
                pe.matmul(to, w0_lo[:, t, :], hi, start=False, stop=(t == TILES - 1)).then_inc(tile_used, 1)

            def add_squares(k):
                pe.wait_ge(square_ready, k + 1)
                pe.matmul(sums[k % 2][:], w0_hi[:, TILES, :], square_parts[:, k % 2, :], start=False, stop=False)\
                    .then_inc(square_used, 1)

            def turn_x1(k):
                pe.wait_ge(sums_stored, k + 1)
                n = ring_no["x1", k]
                free_ring(n)
                for s in range(SUBS):
                    mm = pe.transpose(ring[n % 2][:, P * s:P * s + P], x1[:, P * s:P * s + P], ident_f[:])
                mm.then_inc(ring_full, 1)

            def dot(k, s):
                n = ring_no["dot", k, s]
                pe.wait_ge(ring_low, low_no["x1", k] + 1)
                pe.wait_ge(diag_in[k % 2], 16 * SUB * (k // 2 + 1))
                free_ring(n)
                to = ring[n % 2][:, 0:SUB * WIDE]
                hi, lo = turned_hi[:, k % 2, s, :], turned_lo[:, k % 2, s, :]
                pe.matmul(to, hi, diag[:, k % 2, s, 0, :], start=True, stop=False)
                pe.matmul(to, hi, diag[:, k % 2, s, 1, :], start=False, stop=False)
                pe.matmul(to, lo, diag[:, k % 2, s, 0, :], start=False, stop=True).then_inc(ring_full, 1)

            def second_layer(g, i0, i1):
                for i in range(i0, min(i1, FIELDS)):
                    if i == 0:
                        pe.wait_ge(w1_in, 16)
                        if g:
                            pe.wait_ge(tower_drained, NMLP * g)
                        pe.wait_ge(ring_drained, ring_no["dot", 4 * g + 3, SUBS - 1] + 1)
                    mm = pe.matmul(tower[:, 0:GROUP], w1_sb[:, i, :], dots[:, g % 2, i, :],
                                   start=(i == 0), stop=(i == FIELDS - 1))
                    if i == FIELDS - 1:
                        mm.then_inc(tower_full, 1)

            def tower_step(g, step):
                pe.wait_ge(tower_drained, NMLP * g + step)
                if step == 1:
                    if g == 0:
                        pe.wait_ge(ring_drained, 1)
                    for n in range(H1 // P):
                        to, cols = tower[:, GROUP * n:GROUP * n + GROUP], slice(P * n, P * n + P)
                        pe.matmul(to, wt1_sb[:, 0, cols], dots[:, g % 2, FIELDS, :], start=True, stop=False)
                        pe.matmul(to, wt1_sb[:, 1, cols], z2[:], start=False, stop=False)
                        mm = pe.matmul(to, wtd_sb[:, cols], dense_t[:, GROUP * g:GROUP * g + GROUP],
                                       start=False, stop=True)
                if step == 2:
                    for n in range(H2 // P):
                        for j in range(H1 // P):
                            mm = pe.matmul(tower[:, GROUP * n:GROUP * n + GROUP], wt2_sb[:, j, P * n:P * n + P],
                                           h1[:, j, :], start=(j == 0), stop=(j == H1 // P - 1))
                if step == 3:
                    for j in range(H2 // P):
                        mm = pe.matmul(tower[0:1, 0:GROUP], wt3_sb[:, j:j + 1], h2[:, j, :],
                                       start=(j == 0), stop=(j == H2 // P - 1))
                mm.then_inc(tower_full, 1)

            turn_dense()
            turn_fields(0, 0)
            turn_fields(0, 1)
            for what in copy_order[:4]:
                copy_rows(what)
            fields_by_column(0)
            pe.wait_ge(ready, 9)
            fill = {"field": turn_fields, "columns": fields_by_column, "x1": turn_x1, "dot": dot}
            for k in range(BLOCKS + 1):
                g, kk = divmod(k, GROUP // BLOCK)
                for n, step in enumerate(steps):
                    for what in copies_before.get((k, step), []):
                        copy_rows(what)
                    if k < BLOCKS:
                        if step == "S":
                            add_squares(k)
                        else:
                            add_tile(k, step)
                    for what in ring_after.get((k, step), []):
                        fill[what[0]](*what[1:])
                    if g and kk in (1, 2):
                        at = 3 * (len(steps) * (kk - 1) + n)
                        second_layer(g - 1, at, at + 3)
                    if tower_fills.get((k, step), (0, 0))[1]:
                        tower_step(*tower_fills[k, step])
            second_layer(GROUPS - 1, 0, FIELDS)
            for step in (1, 2, 3):
                tower_step(GROUPS - 1, step)


def kernel(dense_ctx, ids, W_top1, b_top1, W_top2, b_top2, W_top3, L0_rec_W0, L0_rec_W1, **tables):
    import concourse.bacc as bacc
    from concourse.bass_utils import run_bass_kernel_spmd

    tabs = [np.asarray(tables[f"tbl_{i}"]) for i in range(FIELDS)]
    starts = np.cumsum([0] + [t.shape[0] for t in tabs])[:FIELDS]
    offsets = np.zeros((P, HALF), np.int32)
    for i in range(FIELDS):
        offsets[64 * (i // HALF):64 * (i // HALF) + 64, i % HALF] = starts[i]
    sel, back = selections()
    ij, ji = pair_rows()
    w0 = np.concatenate([np.asarray(L0_rec_W0)[0], np.zeros((1, P), np.float32)])
    arrays = {
        "table": np.concatenate(tabs),
        "ids": np.asarray(ids),
        "offsets": offsets,
        "w0_ij": np.ascontiguousarray(w0[ij.T]),
        "w0_ji": np.ascontiguousarray(w0[ji.T]),
        "w1": np.asarray(L0_rec_W1)[0],
        "sel": sel,
        "back": back,
        "ident": np.eye(P, dtype=np.float32),
        "dense": np.asarray(dense_ctx),
        "wt1": np.asarray(W_top1),
        "bt1": np.ascontiguousarray(np.asarray(b_top1).reshape(-1, P).T),
        "wt2": np.asarray(W_top2),
        "bt2": np.ascontiguousarray(np.asarray(b_top2).reshape(-1, P).T),
        "wt3": np.ascontiguousarray(np.asarray(W_top3).reshape(-1, P).T),
    }
    nc = bacc.Bacc("TRN2", target_bir_lowering=False, num_devices=1)
    args = {n: nc.dram_tensor(n, a.shape, mybir.dt.from_np(a.dtype), kind="ExternalInput").ap() for n, a in arrays.items()}
    out = nc.dram_tensor("out", (BATCH, 1), F32, kind="ExternalOutput").ap()
    build(nc, **args, out=out)
    return run_bass_kernel_spmd(nc, [arrays], core_ids=[0]).results[0]["out"]
```

```python
from contextlib import ExitStack

import numpy as np

import concourse.bass as bass
from concourse import mybir

ALU = mybir.AluOpType
ACT = mybir.ActivationFunctionType
F32 = mybir.dt.float32
F32R = mybir.dt.float32r
BF16 = mybir.dt.bfloat16
I32 = mybir.dt.int32
U32 = mybir.dt.uint32

P = 128
FIELDS = 39
DIM = 16
BATCH = 512
BLOCK = 32
QUARTER = 10
BLOCKS = BATCH // BLOCK
GROUP = 128
GROUPS = BATCH // GROUP
COLS = BLOCK * DIM
SUB = P // DIM
SUBS = BLOCK // SUB
WIDE = FIELDS + 1
TILES = 6
LEFT = FIELDS * (FIELDS + 1) // 2 - TILES * P
QUAD = 32
H1, H2 = 512, 256


def first_of_pair():
    return [p % FIELDS for p in range(P)]


def pair_tiles():
    first = first_of_pair()
    room = {i: TILES * first.count(i) for i in range(FIELDS)}
    partners = {i: [i] if i >= LEFT else [] for i in range(FIELDS)}
    need = {i: room[i] - len(partners[i]) for i in range(FIELDS)}
    open_fields = list(range(FIELDS))
    while open_fields:
        open_fields.sort(key=lambda i: (need[i], i))
        v = open_fields.pop(0)
        wins = need[v]
        for n, w in enumerate(open_fields):
            if n < wins:
                partners[v].append(w)
            else:
                partners[w].append(v)
                need[w] -= 1
        assert 0 <= wins <= len(open_fields)
    assert all(len(partners[i]) == room[i] for i in range(FIELDS))
    tiles = []
    for _ in range(TILES):
        tiles.append([partners[i].pop() for i in first])
    return tiles


def part_row(field, part):
    return QUAD * (field // QUARTER) + part * QUARTER + field % QUARTER


def selections():
    sel = np.zeros((P, TILES + 1, P), np.float32)
    back = np.zeros((P, WIDE), np.float32)
    tiles = [first_of_pair(), *pair_tiles()]
    for n, fields in enumerate(tiles):
        for p, i in enumerate(fields):
            for part in range(3):
                sel[part_row(i, part), n, p] = 1
    for i in range(FIELDS):
        for part in range(3):
            back[part_row(i, part), i] = 1
    return sel, back


def pair_rows():
    first, none = first_of_pair(), FIELDS * FIELDS
    ij = np.full((TILES + 1, P), none)
    ji = np.full((TILES + 1, P), none)
    for t, second in enumerate(pair_tiles()):
        for p, (i, j) in enumerate(zip(first, second)):
            ij[t, p] = i * FIELDS + j
            if i != j:
                ji[t, p] = j * FIELDS + i
    for n in range(3):
        for i in range(LEFT):
            ij[TILES, FIELDS * n + i] = i * FIELDS + i
    return ij, ji


NMLP = 4

STEPS = TILES + 1
TENSOR = dict(first=-3.51, second=(-3.43, -3.32, -3.09, -2.19, -1.71, -0.56),
              tile=(-0.0, 1.0, 2.0, 3.0, 4.0, 6.0), sum_squares=5.68, columns=-0.86, x1=8.68,
              dot=(10.74, 10.9, 11.77, 12.05))
SCALAR = dict(first=-2.73, high=(-1.73, -1.71, -0.8, -0.66, 4.2, 4.84), squares=2.8, sums=6.9, columns=0.41,
              x1=10.57, dot=(12.12, 12.27, 13.05, 13.06))
VECTOR = dict(product=(-4.16, -4.1, -3.16, -1.71, -1.14, -0.22), low=(-2.36, -1.86, -1.18, -0.66, 2.03, 3.28),
              squares=2.5, split=(-6.51, -6.31, -5.53, -5.32, -5.15), columns=0.72, x1=8.88)
GROUP_TENSOR = (dict(layer2=6.22, rate=2.58, tower=(23.18, 26.7, 31.41)),
                dict(layer2=6.11, rate=2.84, tower=(24.45, 27.61, 30.02)),
                dict(layer2=6.49, rate=2.72, tower=(22.71, 30.79, 31.9)))
GROUP_SCALAR = ((23.33, 26.23, 29.15, 32.32), (22.1, 26.57, 28.3, 32.76), (21.63, 26.88, 32.35, 75.59))
GROUP_VECTOR = (23.59, 23.68, 25.09)


def orders(tensor=TENSOR, scalar=SCALAR, vector=VECTOR, group_tensor=GROUP_TENSOR, group_scalar=GROUP_SCALAR,
           group_vector=GROUP_VECTOR):
    pe, act, dve = [], [], []
    for k in range(BLOCKS):
        for items, table in ((pe, tensor), (act, scalar), (dve, vector)):
            for name, steps in table.items():
                if isinstance(steps, float):
                    items.append((STEPS * k + steps, (name, k)))
                else:
                    items.extend((STEPS * k + step, (name, k, n)) for n, step in enumerate(steps))
    for g in range(GROUPS - 1):
        end = STEPS * (GROUP // BLOCK) * (g + 1)
        when = group_tensor[g]
        pe.extend((end + when["layer2"] + i / when["rate"], ("layer2", g, i)) for i in range(FIELDS))
        pe.extend((end + step, ("tower", g, n + 1)) for n, step in enumerate(when["tower"]))
        act.extend((end + step, ("tower", g, n)) for n, step in enumerate(group_scalar[g]))
        dve.append((end + group_vector[g], ("h1", g)))
    return [[what for _, what in sorted(items, key=lambda x: x[0])] for items in (pe, act, dve)]


def build(nc, table, ids, w0_ij, w0_ji, w1, sel, back, ident, dense, wt1, bt1, wt2, bt2, wt3, out):
    ctx = ExitStack()
    with ctx:
        def sb(name, shape, dt=F32):
            return ctx.enter_context(nc.sbuf_tensor(name, shape, dt))

        def bank(name, shape=(P, COLS), dt=F32):
            return ctx.enter_context(nc.psum_tensor(name, list(shape), dt))

        def sem(name):
            return ctx.enter_context(nc.semaphore(name))

        NPROD, NPART, NGATHER, NTURN = 5, 7, 3, 3
        pe_order, act_order, dve_order = orders()
        ids_sb = sb("ids_sb", [P, BLOCKS + 1, QUARTER], I32)
        rows = sb("rows", [P, BLOCKS, QUARTER], I32)
        gathered = sb("gathered", [P, NGATHER, QUARTER, DIM])
        rest = sb("rest", [P, QUARTER, DIM])
        parts = sb("parts", [P, 2, DIM // 2, QUAD, 2], BF16)
        turned = sb("turned", [P, NTURN, COLS], BF16)
        sel_f = sb("sel_f", [P, TILES + 1, P])
        sel_sb = sb("sel_sb", [P, TILES + 1, P], BF16)
        back_f = sb("back_f", [P, WIDE])
        back_sb = sb("back_sb", [P, WIDE], BF16)
        ident_f = sb("ident_f", [P, P])
        w0a = sb("w0a", [P, TILES + 1, P])
        w0b = sb("w0b", [P, TILES + 1, P])
        w0_hi = sb("w0_hi", [P, TILES + 1, P], F32R)
        w0_lo = sb("w0_lo", [P, TILES, P], F32R)
        first = sb("first", [P, 2, COLS])
        prod = sb("prod", [P, NPROD, COLS])
        prod_hi = sb("prod_hi", [P, NPART, COLS], F32R)
        prod_lo = sb("prod_lo", [P, NPART, COLS], F32R)
        square = sb("square", [P, 2, COLS])
        square_parts = sb("square_parts", [P, 2, COLS], F32R)
        x1 = sb("x1", [P, COLS])
        turned_hi = sb("turned_hi", [P, 2, SUBS, P], F32R)
        turned_lo = sb("turned_lo", [P, 2, SUBS, P], F32R)
        columns = sb("columns", [P, 2, SUBS, 2, WIDE], F32R)
        diag = sb("diag", [P, 2, SUBS, 2, SUB * WIDE], F32R)
        dots = sb("dots", [P, 2, WIDE, GROUP])
        w1_sb = sb("w1_sb", [P, FIELDS, P])
        dense_sb = sb("dense_sb", [P, GROUPS, DIM])
        dense_t = sb("dense_t", [DIM, BATCH])
        wt1_sb = sb("wt1_sb", [P, 2, H1])
        wtd_sb = sb("wtd_sb", [DIM, H1])
        wt2_sb = sb("wt2_sb", [P, H1 // P, H2])
        wt3_sb = sb("wt3_sb", [P, H2 // P])
        bt1_sb = sb("bt1_sb", [P, H1 // P])
        bt2_sb = sb("bt2_sb", [P, H2 // P])
        z2 = sb("z2", [P, GROUP])
        h1_dense = sb("h1_dense", [P, H1 // P, GROUP * (GROUPS - 1)])
        h1 = sb("h1", [P, H1 // P, GROUP])
        h2 = sb("h2", [P, H2 // P, GROUP])
        y = sb("y", [1, BATCH])

        copies = [bank(f"copies{i}") for i in range(3)]
        sums = [bank(f"sums{i}") for i in range(2)]
        ring = [bank(f"ring{i}") for i in range(2)]
        tower = bank("tower")

        dense_banks = [*sums, tower, sums[0]]
        h1_banks = [*copies, sums[0]]
        h2_banks = [sums[1], ring[0]]
        y_bank = ring[1]

        ids_in = sem("ids_in")
        sel_in = sem("sel_in")
        w0_in = sem("w0_in")
        w1_in = sem("w1_in")
        tower_in = sem("tower_in")
        block_in = [sem(f"block_in{i}") for i in range(NGATHER)]
        diag_in = [sem(f"diag_in{i}") for i in range(2)]
        stored = sem("stored")
        ready = sem("ready")
        missing = sem("missing")
        zeroed = sem("zeroed")
        rows_ready = sem("rows_ready")
        dense_full = sem("dense_full")
        dense_stored = sem("dense_stored")
        rest_step = sem("rest_step")
        parts_ready = sem("parts_ready")
        turned_ready = sem("turned_ready")
        copied = sem("copied")
        first_ready = sem("first_ready")
        prod_ready = sem("prod_ready")
        hi_ready = sem("hi_ready")
        lo_ready = sem("lo_ready")
        tile_used = sem("tile_used")
        squared = sem("squared")
        square_hi = sem("square_hi")
        square_ready = sem("square_ready")
        square_used = sem("square_used")
        sums_stored = sem("sums_stored")
        ring_full = sem("ring_full")
        ring_drained = sem("ring_drained")
        ring_low = sem("ring_low")
        tower_full = sem("tower_full")
        tower_drained = sem("tower_drained")
        h1_summed = sem("h1_summed")
        last_h1_full = sem("last_h1_full")
        last_h1 = sem("last_h1")
        last_h2_full = sem("last_h2_full")
        last_h2 = [sem(f"last_h2_{n}") for n in range(H2 // P)]
        last_y_full = sem("last_y_full")
        last_y = sem("last_y")

        copy_order = [x for x in pe_order if x[0] in ("first", "second")]
        copy_no = {what: n for n, what in enumerate(copy_order)}
        ring_order = [("dense", 0)] + [x for x in pe_order if x[0] in ("columns", "x1", "dot")]
        ring_no = {what: n for n, what in enumerate(ring_order)}
        low_no = {what: n for n, what in enumerate(x for x in ring_order if x[0] in ("columns", "x1"))}

        def by_sub(of):
            return of[:, 0:SUBS * WIDE].rearrange("p (s i) -> p s i", i=WIDE)

        block = ctx.enter_context(nc.Block())

        @block.sync
        def _(sp):
            sp.dma_start(ids_sb[:], ids).then_inc(ids_in, 16)
            sp.dma_start(sel_f[:], sel).then_inc(sel_in, 16)
            sp.dma_start(back_f[:], back).then_inc(sel_in, 16)
            sp.dma_start(ident_f[:], ident).then_inc(sel_in, 16)
            sp.dma_start(w0a[:], w0_ij).then_inc(w0_in, 16)
            sp.dma_start(w0b[:], w0_ji).then_inc(w0_in, 16)
            sp.dma_start(dense_sb[:], dense.rearrange("(g b) d -> b g d", b=GROUP)).then_inc(tower_in, 16)
            sp.dma_start(wt1_sb[:], wt1[0:2 * P, :].rearrange("(k p) n -> p k n", p=P)).then_inc(tower_in, 16)
            sp.dma_start(wtd_sb[:], wt1[2 * P:2 * P + DIM, :]).then_inc(tower_in, 16)
            sp.dma_start(wt2_sb[:], wt2.rearrange("(k p) n -> p k n", p=P)).then_inc(tower_in, 16)
            sp.dma_start(wt3_sb[:], wt3).then_inc(tower_in, 16)
            sp.dma_start(bt1_sb[:], bt1).then_inc(tower_in, 16)
            sp.dma_start(bt2_sb[:], bt2).then_inc(tower_in, 16)
            sp.dma_start(w1_sb[:], w1.rearrange("(i j) h -> j i h", i=FIELDS)).then_inc(w1_in, 16)
            sp.wait_ge(zeroed, 3)
            for k in range(BLOCKS):
                sp.wait_ge(ring_low, low_no["columns", k] + 1)
                if k >= 2:
                    sp.wait_ge(ring_full, ring_no["dot", k - 2, SUBS - 1] + 1)
                for b in range(SUB):
                    sp.dma_start(diag[DIM * b:DIM * b + DIM, k % 2, :, :, WIDE * b:WIDE * b + WIDE].bitcast(F32),
                                 columns[DIM * b:DIM * b + DIM, k % 2, :, :, :].bitcast(F32))\
                        .then_inc(diag_in[k % 2], 16)
            sp.wait_ge(last_y, 1)
            sp.dma_start(out.rearrange("b o -> o b"), y[:]).then_inc(stored, 16)
            sp.wait_ge(stored, 16)

        @block.gpsimd
        def _(pool):
            pool.memset(gathered[3 * QUAD:P, :, QUARTER - 1, :], 0.0).then_inc(missing, 1)
            pool.wait_ge(rows_ready, 1)
            for k in range(BLOCKS):
                if k >= NGATHER:
                    pool.wait_ge(parts_ready, k - NGATHER + 1)
                for q in range(QUARTER):
                    n = P if 3 * QUARTER + q < FIELDS else 3 * QUAD
                    pool.indirect_dma_start(
                        gathered[0:n, k % NGATHER, q, :], None, table,
                        bass.IndirectOffsetOnAxis(ap=rows[0:n, k, q:q + 1], axis=0)).then_inc(block_in[k % NGATHER], 16)

        @block.vector
        def _(dve):
            dve.wait_ge(ids_in, 16)
            nc.vector.tensor_tensor(rows[:], ids_sb[:, 0:BLOCKS, :],
                                    ids_sb[:, BLOCKS:BLOCKS + 1, :].broadcast_to([P, BLOCKS, QUARTER]),
                                    ALU.add).then_inc(rows_ready, 1)
            nc.vector.memset(parts[:, :, :, 3 * QUARTER:QUAD, :], 0.0).then_inc(ready, 1)
            dve.wait_ge(sel_in, 48)
            nc.vector.tensor_copy(sel_sb[:], sel_f[:]).then_inc(ready, 1)
            nc.vector.tensor_copy(back_sb[:], back_f[:]).then_inc(ready, 1)
            dve.wait_ge(w0_in, 32)
            nc.vector.tensor_tensor(w0a[:], w0a[:], w0b[:], ALU.add).then_inc(ready, 1)
            dve.wait_ge(ready, 4)
            nc.vector.tensor_copy(w0_hi[:], w0a[:]).then_inc(ready, 1)
            dve.wait_ge(ready, 5)
            nc.vector.tensor_tensor(w0_lo[:], w0a[:, 0:TILES, :], w0_hi[:, 0:TILES, :], ALU.subtract).then_inc(ready, 1)
            nc.vector.tensor_tensor(w0_hi[QUAD:2 * QUAD, TILES, :], w0a[QUAD:2 * QUAD, TILES, :],
                                    w0_hi[QUAD:2 * QUAD, TILES, :], ALU.subtract).then_inc(ready, 1)
            nc.vector.memset(diag[:].bitcast(F32), 0.0).then_inc(zeroed, 1)
            nc.vector.memset(columns[:, :, :, 0, FIELDS:WIDE].bitcast(F32), 1.0).then_inc(zeroed, 1)
            nc.vector.memset(columns[:, :, :, 1, FIELDS:WIDE].bitcast(F32), 0.0).then_inc(zeroed, 1)

            def split(k, step):
                g = gathered[:, k % NGATHER, :, :].rearrange("p q (e t) -> p e q t", t=2)
                r = rest[:].rearrange("p q (e t) -> p e q t", t=2)
                high, middle, low = (parts[:, k % 2, :, QUARTER * n:QUARTER * n + QUARTER, :] for n in range(3))
                if step == 0:
                    dve.wait_ge(block_in[k % NGATHER], 16 * QUARTER * (k // NGATHER + 1))
                    if k == 0:
                        dve.wait_ge(missing, 1)
                    if k >= 2:
                        dve.wait_ge(turned_ready, k - 1)
                    nc.vector.tensor_copy(high, g).then_inc(rest_step, 1)
                if step == 1:
                    dve.wait_ge(rest_step, 3 * k + 1)
                    nc.vector.tensor_tensor(r, g, high, ALU.subtract).then_inc(rest_step, 1)
                if step == 2:
                    dve.wait_ge(rest_step, 3 * k + 2)
                    nc.vector.tensor_copy(middle, r).then_inc(rest_step, 1)
                if step == 3:
                    dve.wait_ge(rest_step, 3 * k + 3)
                    nc.vector.tensor_tensor(low, r, middle, ALU.subtract).then_inc(parts_ready, 1)
                if step == 4:
                    dve.wait_ge(parts_ready, k + 1)
                    if k >= NTURN:
                        was = k - NTURN
                        dve.wait_ge(copied, copy_no["second", was, TILES - 1] + 1)
                        dve.wait_ge(ring_full, ring_no["columns", was] + 1)
                    nc.vector.transpose(turned[:, k % NTURN, :].bitcast(U32).rearrange("p (b e) -> p e b", b=BLOCK),
                                        parts[:, k % 2, :, :, :].rearrange("p e r t -> p e (r t)").bitcast(U32))\
                        .then_inc(turned_ready, 1)

            def product(k, t):
                m = TILES * k + t
                n = copy_no["second", k, t]
                dve.wait_ge(first_ready, k + 1)
                dve.wait_ge(copied, n + 1)
                if m >= NPROD:
                    dve.wait_ge(lo_ready, m - NPROD + 1)
                nc.vector.tensor_tensor(prod[:, m % NPROD, :], first[:, k % 2, :], copies[n % 3][:], ALU.mult)\
                    .then_inc(prod_ready, 1)

            def low(k, t):
                m = TILES * k + t
                dve.wait_ge(hi_ready, m + 1)
                if m >= NPART:
                    dve.wait_ge(tile_used, m - NPART + 1)
                nc.vector.tensor_tensor(prod_lo[:, m % NPART, :], prod[:, m % NPROD, :],
                                        prod_hi[:, m % NPART, :], ALU.subtract).then_inc(lo_ready, 1)

            def square_low(k):
                dve.wait_ge(square_hi, k + 1)
                half = square_parts[64:P, k % 2, :]
                nc.vector.tensor_tensor(half, square[64:P, k % 2, :], half, ALU.subtract).then_inc(square_ready, 1)

            def columns_low(k):
                n = ring_no["columns", k]
                dve.wait_ge(ring_drained, n + 1)
                if k >= 2:
                    dve.wait_ge(diag_in[k % 2], 16 * SUB * (k // 2))
                nc.vector.tensor_tensor(columns[:, k % 2, :, 1, 0:FIELDS], by_sub(ring[n % 2])[:, :, 0:FIELDS],
                                        columns[:, k % 2, :, 0, 0:FIELDS], ALU.subtract).then_inc(ring_low, 1)

            def h1_sum(g):
                dve.wait_ge(tower_full, NMLP * g + 2)
                if g == 0:
                    dve.wait_ge(dense_stored, H1 // P)
                nc.vector.tensor_tensor(h1[:], tower[:].rearrange("p (n b) -> p n b", b=GROUP),
                                        h1_dense[:, :, GROUP * g:GROUP * g + GROUP], ALU.add).then_inc(h1_summed, 1)

            def turned_low(k):
                n = ring_no["x1", k]
                dve.wait_ge(ring_drained, n + 1)
                if k >= 2:
                    dve.wait_ge(ring_full, ring_no["dot", k - 2, SUBS - 1] + 1)
                nc.vector.tensor_tensor(turned_lo[:, k % 2, :, :], ring[n % 2][:].rearrange("p (s h) -> p s h", h=P),
                                        turned_hi[:, k % 2, :, :], ALU.subtract).then_inc(ring_low, 1)

            for what in dve_order:
                {"split": split, "columns": columns_low, "product": product, "low": low,
                 "squares": square_low, "x1": turned_low, "h1": h1_sum}[what[0]](*what[1:])
            dve.wait_ge(tower_in, 16 * 7)
            dve.wait_ge(last_h2_full, 2)
            nc.vector.tensor_scalar(h2[:, 1, :], h2_banks[1][:, 0:GROUP], bt2_sb[:, 1:2], 0.0,
                                    ALU.add, ALU.max).then_inc(last_h2[1], 1)

        @block.scalar
        def _(act):
            def store_columns(k):
                n = ring_no["columns", k]
                act.wait_ge(ring_full, n + 1)
                if k >= 2:
                    act.wait_ge(diag_in[k % 2], 16 * SUB * (k // 2))
                nc.scalar.copy(columns[:, k % 2, :, 0, 0:FIELDS], by_sub(ring[n % 2])[:, :, 0:FIELDS])\
                    .then_inc(ring_drained, 1)

            def store_first(k):
                n = copy_no["first", k]
                act.wait_ge(copied, n + 1)
                if k >= 2:
                    act.wait_ge(prod_ready, TILES * (k - 1))
                    act.wait_ge(squared, k - 1)
                nc.scalar.copy(first[:, k % 2, :], copies[n % 3][:]).then_inc(first_ready, 1)

            def high(k, t):
                m = TILES * k + t
                act.wait_ge(prod_ready, m + 1)
                if m >= NPART:
                    act.wait_ge(tile_used, m - NPART + 1)
                    act.wait_ge(lo_ready, m - NPART + 1)
                nc.scalar.copy(prod_hi[:, m % NPART, :], prod[:, m % NPROD, :]).then_inc(hi_ready, 1)

            def square_both(k):
                act.wait_ge(first_ready, k + 1)
                if k >= 2:
                    act.wait_ge(square_ready, k - 1)
                    act.wait_ge(square_used, k - 1)
                nc.scalar.activation(square[:, k % 2, :], first[:, k % 2, :], ACT.Square).then_inc(squared, 1)
                act.wait_ge(squared, k + 1)
                nc.scalar.copy(square_parts[:, k % 2, :], square[:, k % 2, :]).then_inc(square_hi, 1)

            def store_x1(k):
                act.wait_ge(tile_used, TILES * (k + 1))
                if k:
                    act.wait_ge(ring_full, ring_no["x1", k - 1] + 1)
                nc.scalar.copy(x1[:], sums[k % 2][:]).then_inc(sums_stored, 1)

            def store_turned(k):
                n = ring_no["x1", k]
                act.wait_ge(ring_full, n + 1)
                if k >= 2:
                    act.wait_ge(ring_full, ring_no["dot", k - 2, SUBS - 1] + 1)
                nc.scalar.copy(turned_hi[:, k % 2, :, :], ring[n % 2][:].rearrange("p (s h) -> p s h", h=P))\
                    .then_inc(ring_drained, 1)

            def store_dots(k, s):
                n = ring_no["dot", k, s]
                g, at = divmod(k * BLOCK + s * SUB, GROUP)
                act.wait_ge(ring_full, n + 1)
                if g >= 2 and at == 0:
                    act.wait_ge(tower_full, NMLP * (g - 2) + 2)
                nc.scalar.copy(dots[:, g % 2, :, at:at + SUB].rearrange("p i b -> p b i"),
                               ring[n % 2][:, 0:SUB * WIDE].rearrange("p (b i) -> p b i", i=WIDE))\
                    .then_inc(ring_drained, 1)

            def tower_step(g, step):
                act.wait_ge(tower_full, NMLP * g + step + 1)
                if step == 0:
                    last = nc.scalar.copy(z2[:], tower[:, 0:GROUP])
                if step == 1:
                    act.wait_ge(h1_summed, g + 1)
                    last = nc.scalar.activation(h1[:], h1[:], ACT.Relu)
                if step == 2:
                    for n in range(H2 // P):
                        last = nc.scalar.activation(h2[:, n, :], tower[:, GROUP * n:GROUP * n + GROUP], ACT.Relu,
                                                    bias=bt2_sb[:, n:n + 1])
                if step == 3:
                    last = nc.scalar.copy(y[:, GROUP * g:GROUP * g + GROUP], tower[0:1, 0:GROUP])
                last.then_inc(tower_drained, 1)

            def store_dense():
                act.wait_ge(ring_full, 1)
                nc.scalar.copy(dense_t[:], ring[0][0:DIM, :]).then_inc(ring_drained, 1)
                for n in range(H1 // P):
                    act.wait_ge(dense_full, n + 1)
                    nc.scalar.activation(h1_dense[:, n, :], dense_banks[n][:, 0:GROUP * (GROUPS - 1)], ACT.Identity,
                                         bias=bt1_sb[:, n:n + 1]).then_inc(dense_stored, 1)

            store_dense()
            for what in act_order:
                {"columns": store_columns, "first": store_first,
                 "high": high, "squares": square_both, "sums": store_x1, "x1": store_turned,
                 "dot": store_dots, "tower": tower_step}[what[0]](*what[1:])
            tower_step(GROUPS - 1, 0)
            for n in range(H1 // P):
                act.wait_ge(last_h1_full, n + 1)
                nc.scalar.activation(h1[:, n, :], h1_banks[n][:, 0:GROUP], ACT.Relu,
                                     bias=bt1_sb[:, n:n + 1]).then_inc(last_h1, 1)
            act.wait_ge(last_h2_full, 1)
            nc.scalar.activation(h2[:, 0, :], h2_banks[0][:, 0:GROUP], ACT.Relu, bias=bt2_sb[:, 0:1]).then_inc(last_h2[0], 1)
            act.wait_ge(last_y_full, 1)
            nc.scalar.copy(y[:, GROUP * (GROUPS - 1):], y_bank[0:1, 0:GROUP]).then_inc(last_y, 1)

        @block.tensor
        def _(pe):
            def free_ring(n):
                if n >= 2:
                    was = ring_order[n - 2]
                    if was in low_no:
                        pe.wait_ge(ring_low, low_no[was] + 1)
                    else:
                        pe.wait_ge(ring_drained, n - 1)

            def turn_dense():
                pe.wait_ge(tower_in, 16 * 7)
                pe.wait_ge(sel_in, 48)
                for g in range(GROUPS):
                    mm = pe.transpose(ring[0][0:DIM, GROUP * g:GROUP * g + GROUP], dense_sb[:, g, :], ident_f[:])
                mm.then_inc(ring_full, 1)
                pe.wait_ge(ring_drained, 1)
                for n in range(H1 // P):
                    if n == len(dense_banks) - 1:
                        pe.wait_ge(dense_stored, 1)
                    pe.matmul(dense_banks[n][:, 0:GROUP * (GROUPS - 1)], wtd_sb[:, P * n:P * n + P],
                              dense_t[:, 0:GROUP * (GROUPS - 1)], start=True, stop=True).then_inc(dense_full, 1)

            def fields_by_column(k):
                pe.wait_ge(turned_ready, k + 1)
                n = ring_no["columns", k]
                free_ring(n)
                for s in range(SUBS):
                    mm = pe.matmul(ring[n % 2][:, WIDE * s:WIDE * s + WIDE], turned[:, k % NTURN, P * s:P * s + P], back_sb[:],
                                   start=True, stop=True)
                mm.then_inc(ring_full, 1)

            def copy_rows(what):
                n = copy_no[what]
                kind, k = what[0:2]
                e = 0 if kind == "first" else 1 + what[-1]
                if kind == "first":
                    pe.wait_ge(turned_ready, k + 1)
                if n >= 3:
                    was = copy_order[n - 3]
                    if was[0] == "first":
                        pe.wait_ge(first_ready, was[1] + 1)
                    else:
                        pe.wait_ge(prod_ready, TILES * was[1] + was[2] + 1)
                pe.matmul(copies[n % 3][:], sel_sb[:, e, :], turned[:, k % NTURN, :],
                          start=True, stop=True).then_inc(copied, 1)

            def add_tile(k, t):
                m = TILES * k + t
                if t == 0:
                    pe.wait_ge(ready, 7)
                    if k == 0:
                        pe.wait_ge(dense_stored, H1 // P)
                if t == 0 and k >= 2:
                    pe.wait_ge(sums_stored, k - 1)
                pe.wait_ge(lo_ready, m + 1)
                hi, lo = prod_hi[:, m % NPART, :], prod_lo[:, m % NPART, :]
                to = sums[k % 2][:]
                pe.matmul(to, w0_hi[:, t, :], hi, start=(t == 0), stop=False)
                pe.matmul(to, w0_hi[:, t, :], lo, start=False, stop=False)
                pe.matmul(to, w0_lo[:, t, :], hi, start=False, stop=(t == TILES - 1)).then_inc(tile_used, 1)

            def add_squares(k):
                pe.wait_ge(square_ready, k + 1)
                pe.matmul(sums[k % 2][:], w0_hi[:, TILES, :], square_parts[:, k % 2, :], start=False, stop=False)\
                    .then_inc(square_used, 1)

            def turn_x1(k):
                pe.wait_ge(sums_stored, k + 1)
                n = ring_no["x1", k]
                free_ring(n)
                for s in range(SUBS):
                    mm = pe.transpose(ring[n % 2][:, P * s:P * s + P], x1[:, P * s:P * s + P], ident_f[:])
                mm.then_inc(ring_full, 1)

            def dot(k, s):
                n = ring_no["dot", k, s]
                pe.wait_ge(ring_low, low_no["x1", k] + 1)
                pe.wait_ge(diag_in[k % 2], 16 * SUB * (k // 2 + 1))
                free_ring(n)
                to = ring[n % 2][:, 0:SUB * WIDE]
                hi, lo = turned_hi[:, k % 2, s, :], turned_lo[:, k % 2, s, :]
                pe.matmul(to, hi, diag[:, k % 2, s, 0, :], start=True, stop=False)
                pe.matmul(to, hi, diag[:, k % 2, s, 1, :], start=False, stop=False)
                pe.matmul(to, lo, diag[:, k % 2, s, 0, :], start=False, stop=True).then_inc(ring_full, 1)

            def second_layer(g, i):
                if i == 0:
                    pe.wait_ge(w1_in, 16)
                    if g:
                        pe.wait_ge(tower_drained, NMLP * g)
                    pe.wait_ge(ring_drained, ring_no["dot", 4 * g + 3, SUBS - 1] + 1)
                mm = pe.matmul(tower[:, 0:GROUP], w1_sb[:, i, :], dots[:, g % 2, i, :],
                               start=(i == 0), stop=(i == FIELDS - 1))
                if i == FIELDS - 1:
                    mm.then_inc(tower_full, 1)

            def tower_step(g, step):
                pe.wait_ge(tower_drained, NMLP * g + step)
                if step == 1:
                    for n in range(H1 // P):
                        to, cols = tower[:, GROUP * n:GROUP * n + GROUP], slice(P * n, P * n + P)
                        pe.matmul(to, wt1_sb[:, 0, cols], dots[:, g % 2, FIELDS, :], start=True, stop=False)
                        mm = pe.matmul(to, wt1_sb[:, 1, cols], z2[:], start=False, stop=True)
                if step == 2:
                    for n in range(H2 // P):
                        for j in range(H1 // P):
                            mm = pe.matmul(tower[:, GROUP * n:GROUP * n + GROUP], wt2_sb[:, j, P * n:P * n + P],
                                           h1[:, j, :], start=(j == 0), stop=(j == H1 // P - 1))
                if step == 3:
                    for j in range(H2 // P):
                        mm = pe.matmul(tower[0:1, 0:GROUP], wt3_sb[:, j:j + 1], h2[:, j, :],
                                       start=(j == 0), stop=(j == H2 // P - 1))
                mm.then_inc(tower_full, 1)

            def last_first_layer(n):
                to, cols = h1_banks[n][:, 0:GROUP], slice(P * n, P * n + P)
                pe.matmul(to, wt1_sb[:, 0, cols], dots[:, (GROUPS - 1) % 2, FIELDS, :], start=True, stop=False)
                pe.matmul(to, wtd_sb[:, cols], dense_t[:, GROUP * (GROUPS - 1):], start=False, stop=False)

            turn_dense()
            for what in pe_order:
                if what[0] in ("first", "second"):
                    copy_rows(what)
                else:
                    {"columns": fields_by_column,
                     "tile": add_tile, "sum_squares": add_squares, "x1": turn_x1, "dot": dot,
                     "layer2": second_layer, "tower": tower_step}[what[0]](*what[1:])
            pe.wait_ge(prod_ready, TILES * BLOCKS)
            pe.wait_ge(first_ready, BLOCKS)
            pe.wait_ge(sums_stored, BLOCKS)
            pe.wait_ge(ring_drained, ring_no["dot", BLOCKS - 1, SUBS - 1] + 1)
            last_first_layer(0)
            last_first_layer(1)
            for i in range(FIELDS):
                second_layer(GROUPS - 1, i)
            last_first_layer(2)
            last_first_layer(3)
            pe.wait_ge(tower_drained, NMLP * (GROUPS - 1) + 1)
            for n in range(H1 // P):
                pe.matmul(h1_banks[n][:, 0:GROUP], wt1_sb[:, 1, P * n:P * n + P], z2[:],
                          start=False, stop=True).then_inc(last_h1_full, 1)
            for j in range(H1 // P - 1):
                pe.wait_ge(last_h1, j + 1)
                for n in range(H2 // P):
                    pe.matmul(h2_banks[n][:, 0:GROUP], wt2_sb[:, j, P * n:P * n + P], h1[:, j, :],
                              start=(j == 0), stop=False)
            pe.wait_ge(last_h1, H1 // P)
            for n in range(H2 // P):
                pe.matmul(h2_banks[n][:, 0:GROUP], wt2_sb[:, H1 // P - 1, P * n:P * n + P],
                          h1[:, H1 // P - 1, :], start=False, stop=True).then_inc(last_h2_full, 1)
            for j in range(H2 // P):
                pe.wait_ge(last_h2[j], 1)
                mm = pe.matmul(y_bank[0:1, 0:GROUP], wt3_sb[:, j:j + 1], h2[:, j, :],
                               start=(j == 0), stop=(j == H2 // P - 1))
            mm.then_inc(last_y_full, 1)


def kernel(dense_ctx, ids, W_top1, b_top1, W_top2, b_top2, W_top3, L0_rec_W0, L0_rec_W1, **tables):
    import concourse.bacc as bacc
    from concourse.bass_utils import run_bass_kernel_spmd

    tabs = [np.asarray(tables[f"tbl_{i}"]) for i in range(FIELDS)]
    starts = np.cumsum([0] + [t.shape[0] for t in tabs])[:FIELDS]
    indices = np.zeros((4, BLOCK, BLOCKS + 1, QUARTER), np.int32)
    for f in range(4):
        n = min(QUARTER, FIELDS - QUARTER * f)
        of = np.asarray(ids)[:, QUARTER * f:QUARTER * f + n]
        indices[f, :, :BLOCKS, :n] = of.reshape(BLOCKS, BLOCK, n).transpose(1, 0, 2)
        indices[f, :, BLOCKS, :n] = starts[QUARTER * f:QUARTER * f + n]
    sel, back = selections()
    ij, ji = pair_rows()
    w0 = np.concatenate([np.asarray(L0_rec_W0)[0], np.zeros((1, P), np.float32)])
    arrays = {
        "table": np.concatenate(tabs),
        "ids": indices.reshape(P, BLOCKS + 1, QUARTER),
        "w0_ij": np.ascontiguousarray(w0[ij.T]),
        "w0_ji": np.ascontiguousarray(w0[ji.T]),
        "w1": np.asarray(L0_rec_W1)[0],
        "sel": sel,
        "back": back,
        "ident": np.eye(P, dtype=np.float32),
        "dense": np.asarray(dense_ctx),
        "wt1": np.asarray(W_top1),
        "bt1": np.ascontiguousarray(np.asarray(b_top1).reshape(-1, P).T),
        "wt2": np.asarray(W_top2),
        "bt2": np.ascontiguousarray(np.asarray(b_top2).reshape(-1, P).T),
        "wt3": np.ascontiguousarray(np.asarray(W_top3).reshape(-1, P).T),
    }
    nc = bacc.Bacc("TRN2", target_bir_lowering=False, num_devices=1)
    args = {n: nc.dram_tensor(n, a.shape, mybir.dt.from_np(a.dtype), kind="ExternalInput").ap() for n, a in arrays.items()}
    out = nc.dram_tensor("out", (BATCH, 1), F32, kind="ExternalOutput").ap()
    build(nc, **args, out=out)
    return run_bass_kernel_spmd(nc, [arrays], core_ids=[0]).results[0]["out"]
```
